# Optimizing a Trainium2 kernel written in Bass

```python
import numpy as np
import jax
import jax.numpy as jnp

def _softmax(x, axis=-1):
    return jax.nn.softmax(x, axis=axis)

def _gelu(x):
    return jax.nn.gelu(x, approximate=True)

def _silu(x):
    return jax.nn.silu(x)

def _sigmoid(x):
    return jax.nn.sigmoid(x)

def _layernorm(x, axis=-1, eps=1e-05):
    m = jnp.mean(x, axis=axis, keepdims=True)
    v = jnp.var(x, axis=axis, keepdims=True)
    return (x - m) / jnp.sqrt(v + eps)

def _scatter_add(tgt, idx, src, axis=0):
    return tgt.at[idx].add(src)

def _segment_sum(src, seg, n):
    return jax.ops.segment_sum(src, seg, n)
kernel_name = 'mk_seq_preln_d1_jaxref_r4_0068f0'

def setup_inputs(seed: int=0):
    np.random.seed(seed)
    _w = jnp.asarray

    def _L0_attn_setup():
        import jax, jax.numpy as jnp
        import numpy as np
        D_MODEL = 256
        D_STATE = 16
        LN_EPS = 1e-05
        key = jax.random.key(seed)
        ks = jax.random.split(key, 10)
        B, L, D, N = (4, 256, D_MODEL, D_STATE)
        s = lambda fan_in: 1.0 / np.sqrt(fan_in)
        x_in = jax.random.normal(ks[0], (B, L, D), dtype=jnp.float32)
        W_in = jax.random.uniform(ks[1], (D, 2 * D), jnp.float32, -s(D), s(D))
        W_x = jax.random.uniform(ks[2], (D, D + 2 * N), jnp.float32, -s(D), s(D))
        W_dt = jax.random.uniform(ks[3], (D, D), jnp.float32, -s(D), s(D))
        b_dt = jax.random.uniform(ks[4], (D,), jnp.float32, -4.0, -1.0)
        A_log = jnp.tile(jnp.log(jnp.arange(1, N + 1, dtype=jnp.float32))[None, :], (D, 1))
        D_param = jnp.ones((D,), dtype=jnp.float32)
        W_out = jax.random.uniform(ks[5], (D, D), jnp.float32, -s(D), s(D))
        ln_g = jnp.ones((D,), dtype=jnp.float32)
        ln_b = jnp.zeros((D,), dtype=jnp.float32)
        return {'x_in': x_in, 'W_in': W_in, 'W_x': W_x, 'W_dt': W_dt, 'b_dt': b_dt, 'A_log': A_log, 'D_param': D_param, 'W_out': W_out, 'ln_g': ln_g, 'ln_b': ln_b}
    _L0_attn_in = _L0_attn_setup()

    def _L0_ffn_setup():
        import jax, jax.numpy as jnp
        import numpy as np
        DIM = 256

        def _reference_tuple_inner(x, W_r, W_k, W_v, mu_r, mu_k):
            B, T, C = x.shape
            x_prev = jnp.concatenate([jnp.zeros((B, 1, C), x.dtype), x[:, :-1, :]], axis=1)
            xr = mu_r * x + (1.0 - mu_r) * x_prev
            xk = mu_k * x + (1.0 - mu_k) * x_prev
            r = jax.nn.sigmoid(jnp.einsum('btc,dc->btd', xr, W_r))
            k = jnp.einsum('btc,dc->btd', xk, W_k)
            k_act = jnp.square(jax.nn.relu(k))
            out = r * jnp.einsum('btc,dc->btd', k_act, W_v)
            new_state = x[:, -1, :]
            return (out, new_state)
        key = jax.random.key(seed)
        ks = jax.random.split(key, 6)
        B, T, C = (8, 512, DIM)
        x = jax.random.normal(ks[0], (B, T, C), dtype=jnp.float32)
        s = 1.0 / np.sqrt(C)
        W_r = jax.random.uniform(ks[1], (C, C), jnp.float32, -s, s)
        W_k = jax.random.uniform(ks[2], (C, C), jnp.float32, -s, s)
        W_v = jax.random.uniform(ks[3], (C, C), jnp.float32, -s, s)
        mu_r = jax.random.uniform(ks[4], (C,), jnp.float32)
        mu_k = jax.random.uniform(ks[5], (C,), jnp.float32)
        return {'x': x, 'W_r': W_r, 'W_k': W_k, 'W_v': W_v, 'mu_r': mu_r, 'mu_k': mu_k}
    _L0_ffn_in = _L0_ffn_setup()
    _d = {'L0_attn_x_in': _L0_attn_in['x_in'], 'L0_attn_W_in': _L0_attn_in['W_in'], 'L0_attn_W_x': _L0_attn_in['W_x'], 'L0_attn_W_dt': _L0_attn_in['W_dt'], 'L0_attn_b_dt': _L0_attn_in['b_dt'], 'L0_attn_A_log': _L0_attn_in['A_log'], 'L0_attn_D_param': _L0_attn_in['D_param'], 'L0_attn_W_out': _L0_attn_in['W_out'], 'L0_attn_ln_g': _L0_attn_in['ln_g'], 'L0_attn_ln_b': _L0_attn_in['ln_b'], 'L0_ffn_W_r': _L0_ffn_in['W_r'], 'L0_ffn_W_k': _L0_ffn_in['W_k'], 'L0_ffn_W_v': _L0_ffn_in['W_v'], 'L0_ffn_mu_r': _L0_ffn_in['mu_r'], 'L0_ffn_mu_k': _L0_ffn_in['mu_k']}
    _x0 = _d['L0_attn_x_in']
    _d['L0_attn_x_in'] = jax.random.normal(jax.random.fold_in(jax.random.key(seed), 1), (4, 2048, 256), dtype=_x0.dtype)
    del _x0
    return _d

def reference(L0_attn_x_in, L0_attn_W_in, L0_attn_W_x, L0_attn_W_dt, L0_attn_b_dt, L0_attn_A_log, L0_attn_D_param, L0_attn_W_out, L0_attn_ln_g, L0_attn_ln_b, L0_ffn_W_r, L0_ffn_W_k, L0_ffn_W_v, L0_ffn_mu_r, L0_ffn_mu_k):

    def _L0_attn_ref(x_in, W_in, W_x, W_dt, b_dt, A_log, D_param, W_out, ln_g, ln_b):
        import jax, jax.numpy as jnp
        import numpy as np
        D_MODEL = 256
        D_STATE = 16
        LN_EPS = 1e-05
        B, L, D = x_in.shape
        N = A_log.shape[1]
        xz = x_in @ W_in
        x, z = (xz[..., :D], xz[..., D:])
        proj = x @ W_x
        delta_raw = proj[..., :D]
        B_ssm = proj[..., D:D + N]
        C_ssm = proj[..., D + N:]
        delta = jax.nn.softplus(delta_raw @ W_dt + b_dt)
        A = -jnp.exp(A_log)
        dA = jnp.exp(jnp.einsum('bld,dn->bldn', delta, A))
        dBx = jnp.einsum('bld,bln->bldn', delta * x, B_ssm)

        def step(h, inp):
            dA_t, dBx_t, C_t = inp
            h = dA_t * h + dBx_t
            y_t = jnp.einsum('bdn,bn->bd', h, C_t)
            return (h, y_t)
        h0 = jnp.zeros((B, D, N), dtype=x.dtype)
        xs = (jnp.moveaxis(dA, 1, 0), jnp.moveaxis(dBx, 1, 0), jnp.moveaxis(C_ssm, 1, 0))
        _, ys = jax.lax.scan(step, h0, xs)
        y = jnp.moveaxis(ys, 0, 1) + x * D_param
        y = y * jax.nn.silu(z) @ W_out
        res = y + x_in
        mu = jnp.mean(res, axis=-1, keepdims=True)
        var = jnp.var(res, axis=-1, keepdims=True)
        return (res - mu) * jax.lax.rsqrt(var + LN_EPS) * ln_g + ln_b

    def _L0_ffn_ref(x, W_r, W_k, W_v, mu_r, mu_k):
        import jax, jax.numpy as jnp
        import numpy as np
        DIM = 256

        def _reference_tuple_inner(x, W_r, W_k, W_v, mu_r, mu_k):
            B, T, C = x.shape
            x_prev = jnp.concatenate([jnp.zeros((B, 1, C), x.dtype), x[:, :-1, :]], axis=1)
            xr = mu_r * x + (1.0 - mu_r) * x_prev
            xk = mu_k * x + (1.0 - mu_k) * x_prev
            r = jax.nn.sigmoid(jnp.einsum('btc,dc->btd', xr, W_r))
            k = jnp.einsum('btc,dc->btd', xk, W_k)
            k_act = jnp.square(jax.nn.relu(k))
            out = r * jnp.einsum('btc,dc->btd', k_act, W_v)
            new_state = x[:, -1, :]
            return (out, new_state)
        return _reference_tuple_inner(x, W_r, W_k, W_v, mu_r, mu_k)[0]
    x = L0_attn_x_in
    x = x + _L0_attn_ref(_layernorm(x, axis=-1), L0_attn_W_in, L0_attn_W_x, L0_attn_W_dt, L0_attn_b_dt, L0_attn_A_log, L0_attn_D_param, L0_attn_W_out, L0_attn_ln_g, L0_attn_ln_b)
    x = x + _L0_ffn_ref(_layernorm(x, axis=-1), L0_ffn_W_r, L0_ffn_W_k, L0_ffn_W_v, L0_ffn_mu_r, L0_ffn_mu_k)
    return x

_drawn_inputs = setup_inputs


def setup_inputs(seed=0):
    import zlib

    import numpy as np

    out = dict(_drawn_inputs(seed))
    spreads = {'L0_attn_D_param': (1.0, 0.6), 'L0_attn_ln_g': (1.0, 0.2), 'L0_attn_ln_b': (0.0, 0.1)}
    factors = {'L0_attn_W_x': 8.0,
     'L0_attn_W_dt': 8.0,
     'L0_attn_b_dt': 8.0,
     'L0_attn_A_log': 8.0,
     'L0_ffn_W_r': 6.442,
     'L0_ffn_mu_r': 8.0}
    for name, (base, spread) in spreads.items():
        noise = np.random.default_rng([zlib.crc32(name.encode()), seed]).standard_normal(out[name].shape)
        drawn = base * np.exp(spread * noise) if base else spread * noise
        out[name] = jnp.asarray(drawn.astype(out[name].dtype))
    for name, factor in factors.items():
        out[name] = (out[name] * factor).astype(out[name].dtype)
    return out
```

```python
from contextlib import ExitStack

import concourse.bass as bass
from concourse import mybir

P = 128
BATCH, LEN, D = 4, 2048, 256
NS = 16
LC = 512
TB = LC // P
KH = D // P
CPB = LEN // LC
NT = BATCH * CPB
EPS = 1e-5
GN = 4
GROUPS = NS // GN
BG = 2
RING = 4
DA_BANKS = 4

F32 = mybir.dt.float32
ALU = mybir.AluOpType
ACT = mybir.ActivationFunctionType

POOL_COLS = [n for n in range(NS) if n % 2 == 1]
VEC_COLS = [n for n in range(NS) if n % 2 == 0]


def made(cols, n):
    return sum(c <= n for c in cols)


def need(eng, sem, count):
    if not (isinstance(count, int) and count <= 0):
        eng.wait_ge(sem, count)


def mamba_rwkv_layer(nc, x_in, W_in, W_x, W_dt, b_dt, A_log, D_param, W_out, ln_g, ln_b,
                     W_r, W_k, W_v, mu_r, mu_k, out):
    x_v = x_in.rearrange("b (c j p) d -> (b c) p j d", p=P, j=TB)
    out_v = out.rearrange("b (c j p) d -> (b c) p j d", p=P, j=TB)
    bc_dram = nc.dram_tensor("bc_rows_dram", (NT, 2 * NS, LC), F32).ap()

    def halves(w):
        return w.rearrange("(k p) n -> p k n", p=P)

    def column(v):
        return v.rearrange("(k p) -> p k", p=P)

    with ExitStack() as ctx:
        def sb(name, *shape):
            return ctx.enter_context(nc.sbuf_tensor(name, list(shape), F32))

        def ps(name, *shape):
            return ctx.enter_context(nc.psum_tensor(name, list(shape), F32))

        def sem(name):
            return ctx.enter_context(nc.semaphore(name))

        ident = sb("ident", P, P)
        w_in = sb("w_in", P, KH, 2 * D)
        w_bc = sb("w_bc", P, KH, 2 * NS)
        w_dtx = sb("w_dtx", P, KH, D)
        w_out = sb("w_out", P, KH, D)
        w_rT = sb("w_rT", P, KH, D)
        w_kT = sb("w_kT", P, KH, D)
        w_vT = sb("w_vT", P, KH, D)
        bdt = sb("bdt", P, KH)
        a_neg = sb("a_neg", P, KH, NS)
        d_par = sb("d_par", P, KH)
        mur = sb("mur", P, KH)
        muk = sb("muk", P, KH)
        omr = sb("omr", P, KH)
        omk = sb("omk", P, KH)
        g_all = sb("g_all", P, D)
        b_all = sb("b_all", P, D)
        notfirst = sb("notfirst", P, NT)
        neg_half = sb("neg_half", P, TB)
        eps_tile = sb("eps_tile", P, TB)
        x_tok = sb("x_tok", P, TB, D)
        xn_tok = sb("xn_tok", P, 2, TB, D)
        xnT = sb("xnT", P, KH, LC)
        xT = sb("xT", P, 2, KH, LC)
        zs = sb("zs", P, 2, KH, LC)
        bc_rows = sb("bc_rows", 2 * NS, LC)
        relu_v = sb("relu_v", P, KH, LC)
        ln_v = sb("ln_v", P, KH, LC)
        one_e = sb("one_e", P, KH, LC)
        abs_v = xnT
        delta = sb("delta", P, 2, KH, LC)
        u = sb("u", P, 2, KH, LC)
        st1 = sb("st1", P, TB, 6)
        mv1 = sb("mv1", P, TB, 2)
        rs1 = sb("rs1", P, TB)
        nm1 = sb("nm1", P, TB)
        b_ring = sb("b_ring", P, BG, GN, LC)
        c_ring = sb("c_ring", P, BG, GN, LC)
        dbx = sb("dbx", P, RING, KH, LC)
        hg = sb("hg", P, RING, KH, LC)
        carry = sb("carry", P, NS, KH)
        xres = sb("xres", P, 2, TB, D)
        gated = sb("gated", P, KH, LC)
        res = sb("res", P, TB, D)
        st2 = sb("st2", P, TB, 6)
        mv2 = sb("mv2", P, TB, 2)
        rs2 = sb("rs2", P, TB)
        nm2 = sb("nm2", P, TB)
        st3 = sb("st3", P, TB, 6)
        mv3 = sb("mv3", P, TB, 2)
        rs3 = sb("rs3", P, TB)
        nm3 = sb("nm3", P, TB)
        hT = sb("hT", P, KH, LC + 1)
        xr = sb("xr", P, KH, LC)
        xk = sb("xk", P, KH, LC)
        kact = sb("kact", P, KH, LC)
        r_out = sb("r_out", P, TB, D)
        wx_raw = c_ring[:, 0, 0:1, :].rearrange("p a (k n) -> p (a k) n", k=KH)
        wdt_raw = c_ring[:, 0, 1:2, :].rearrange("p a (k n) -> p (a k) n", k=KH)
        wxT = c_ring[:, 0, 2:3, :].rearrange("p a (k n) -> p (a k) n", k=KH)
        raw = [b_ring[:, 0, m:m + 1, :].rearrange("p a (k n) -> p (a k) n", k=KH) for m in range(3)]

        y_ps = ps("y_ps", P, KH, LC)
        da_ps = ps("da_ps", P, DA_BANKS, LC)
        pre_ps = ps("pre_ps", P, LC)
        post_ps = ps("post_ps", P, LC)
        post_tok = post_ps[:, :].rearrange("p (s d) -> p s d", d=D)

        names = """w_loaded ident0 ident_done flags0 flags_done half_done a_exped const_done dve_waited sp_waited setup_pe setup_ev
            x_loaded xres_loaded bc_stored out_stored
            ln1_stat ln1_mv ln1_ve ln1_rs ln1_nm xn_done pre_ready pre_read bc_rows_done
            abs_done exp_done ln_done nc_done rl_done delta_done u_done
            carry_in scan_done carry_saved da_ready dbx_vec dbx_pool g_ready y_added
            y_read yd_done gated_done post_ready post_read res_done
            ln2_stat ln2_mv ln2_ve ln2_rs ln2_nm ln2_norm ln2_g ln2_b x2_done
            ln3_stat ln3_mv ln3_ve ln3_rs ln3_nm hn_done prev_done hT_done mixed_prev mixed
            relu_k kact_done sig_done rv_done ffn_done""".split()
        s = {name: sem(name) for name in names}
        b_loaded = [sem(f"b_loaded{g}") for g in range(GROUPS)]
        c_loaded = [sem(f"c_loaded{g}") for g in range(GROUPS)]
        block = ctx.enter_context(nc.Block())

        PRE = ["xnT0", "xnT1", "x0", "x1", "z0", "z1", "bc", "dt0", "dt1"]
        POST_A = ["wo0", "wo1", "hT0", "hT1"]
        POST_B = ["k0", "k1", "r0", "r1", "v0", "v1"]

        def pre_count(i, unit):
            return len(PRE) * i + PRE.index(unit) + 1

        n_post = len(POST_A) + len(POST_B)
        slot_post = ["k0", "k1", "wo0", "wo1", "r0", "r1", "v0", "v1", "hT0", "hT1"]

        def post_count(t, unit):
            if isinstance(t, int) and t == 1:
                return POST_A.index(unit) + 1
            if isinstance(t, int) and t == NT + 1:
                return len(POST_A) + n_post * (NT - 1) + POST_B.index(unit) + 1
            return n_post * (t - 2) + len(POST_A) + slot_post.index(unit) + 1

        def steps(eng, step):
            step(-1, 1, pre=True)
            step(0, 0, pre=True, scan=True)
            step(1, 1, pre=True, scan=True, mid=True)
            with eng.Fori(0, (NT - 4) // 2) as pair:
                step(2 * pair + 2, 0, pre=True, scan=True, mid=True, end=True)
                step(2 * pair + 3, 1, pre=True, scan=True, mid=True, end=True)
            step(NT - 2, 0, pre=True, scan=True, mid=True, end=True)
            step(NT - 1, 1, scan=True, mid=True, end=True)
            step(NT, 0, mid=True, end=True)
            step(NT + 1, 1, end=True)

        @block.sync
        def _(sp):
            loads = [(w_in[:, :, :], halves(W_in)),
                     (w_bc[:, :, :], halves(W_x)[:, :, D:]),
                     (wx_raw, halves(W_x)[:, :, 0:D]),
                     (wdt_raw, halves(W_dt)),
                     (w_out[:, :, :], halves(W_out)),
                     (raw[0], halves(W_r)), (raw[1], halves(W_k)), (raw[2], halves(W_v)),
                     (a_neg[:, :, :], halves(A_log))]
            loads += [(dst[:, :], v.rearrange("(o d) -> o d", o=1).partition_broadcast(P))
                      for dst, v in ((g_all, ln_g), (b_all, ln_b))]
            for dst, v in ((bdt, b_dt), (d_par, D_param), (mur, mu_r), (muk, mu_k)):
                sp.dma_start(dst[:, :], column(v), allow_slow_non_contiguous=True).then_inc(s["w_loaded"], 16)
            for dst, src in loads:
                sp.dma_start(dst, src).then_inc(s["w_loaded"], 16)
            sp.dma_start(x_tok[:, :, :], x_v[0]).then_inc(s["x_loaded"], 16)

            def arrived(sem, count):
                need(sp, sem, count)
                sp.sem_inc(s["sp_waited"], 1)

            def load_group(i, g, first=False):
                if g == 0:
                    arrived(s["bc_stored"], 16 * (i + 1))
                before, at = (i, g - BG) if g >= BG else (i - 1, g + BG)
                if not first:
                    last = GN * at + GN - 1
                    arrived(s["dbx_vec"], len(VEC_COLS) * before + made(VEC_COLS, last))
                    arrived(s["dbx_pool"], len(POOL_COLS) * before + made(POOL_COLS, last))
                sp.dma_start(b_ring[:, g % BG, :, :],
                             bc_dram[i, GN * g:GN * g + GN, :].partition_broadcast(P)).then_inc(b_loaded[g], 16)
                if not first:
                    arrived(s["g_ready"], NS * before + GN * at + GN)
                sp.dma_start(c_ring[:, g % BG, :, :],
                             bc_dram[i, NS + GN * g:NS + GN * g + GN, :].partition_broadcast(P)).then_inc(c_loaded[g], 16)

            def step(t, par, pre=False, scan=False, mid=False, end=False):
                if mid:
                    arrived(s["ffn_done"], t - 2)
                    arrived(s["x2_done"], t - 1)
                    sp.dma_start(xres[:, 1 - par, :, :], x_v[t - 1]).then_inc(s["xres_loaded"], 16)
                if pre and not (isinstance(t, int) and t == NT - 2):
                    arrived(s["xn_done"], t + 2)
                    sp.dma_start(x_tok[:, :, :], x_v[t + 2]).then_inc(s["x_loaded"], 16)
                if scan:
                    for g in range(BG, GROUPS):
                        load_group(t, g)
                if end:
                    arrived(s["ffn_done"], t - 1)
                    sp.dma_start(out_v[t - 2], r_out[:, :, :]).then_inc(s["out_stored"], 16)
                if pre:
                    arrived(s["bc_rows_done"], t + 2)
                    sp.dma_start(bc_dram[t + 1], bc_rows[:, :]).then_inc(s["bc_stored"], 16)
                    if isinstance(t, int) and t == -1:
                        arrived(s["setup_ev"], 5)
                    for g in range(BG):
                        load_group(t + 1, g, first=isinstance(t, int) and t == -1)

            steps(sp, step)
            sp.wait_ge(s["out_stored"], 16 * NT)

        @block.gpsimd
        def _(pool):
            pool.memset(ident[:, :], 0.0).then_inc(s["ident0"], 1)
            pool.wait_ge(s["ident0"], 1)
            pool.affine_select(out=ident[:, :], in_=ident[:, :], compare_op=ALU.not_equal, fill=1.0, base=0,
                               pattern=[[-1, P]], channel_multiplier=1).then_inc(s["ident_done"], 1)

            pool.memset(eps_tile[:, :], EPS).then_inc(s["half_done"], 1)
            pool.memset(neg_half[:, :], -0.5).then_inc(s["half_done"], 1)
            pool.wait_ge(s["half_done"], 2)

            def rsqrt(var, rs, mv_sem, ve_sem, rs_sem, count):
                need(pool, s[mv_sem], count)
                pool.tensor_tensor(rs[:, :], var, eps_tile[:, :], ALU.add).then_inc(s[ve_sem], 1)
                need(pool, s[ve_sem], count)
                pool.tensor_tensor(rs[:, :], rs[:, :], neg_half[:, :], ALU.pow).then_inc(s[rs_sem], 1)

            def times_b(t, par, n):
                if n % GN == POOL_COLS[0]:
                    need(pool, b_loaded[n // GN], 16 * (t + 1))
                if n == POOL_COLS[0]:
                    need(pool, s["u_done"], t + 1)
                need(pool, s["scan_done"], 2 * NS * t + KH * (n - RING + 1))
                pool.tensor_tensor(dbx[:, n % RING, :, :], u[:, par, :, :],
                                   b_ring[:, n // GN % BG, n % GN:n % GN + 1, :].to_broadcast([P, KH, LC]),
                                   ALU.mult).then_inc(s["dbx_pool"], 1)

            def step(t, par, pre=False, scan=False, mid=False, end=False):
                for n in range(NS):
                    if scan:
                        if n + 1 in POOL_COLS:
                            times_b(t, par, n + 1)
                        if n % GN == 0:
                            need(pool, c_loaded[n // GN], 16 * (t + 1))
                        need(pool, s["carry_saved"], NS * t + n + 1)
                        pool.tensor_tensor(hg[:, n % RING, :, :], hg[:, n % RING, :, :],
                                           c_ring[:, n // GN % BG, n % GN:n % GN + 1, :].to_broadcast([P, KH, LC]),
                                           ALU.mult).then_inc(s["g_ready"], 1)
                    if pre and n == 2:
                        rsqrt(mv1[:, :, 1], rs1, "ln1_mv", "ln1_ve", "ln1_rs", t + 2)
                    if mid and n == 5:
                        rsqrt(mv2[:, :, 1], rs2, "ln2_mv", "ln2_ve", "ln2_rs", t)
                    if mid and n == 7:
                        need(pool, s["ln2_norm"], t)
                        pool.tensor_tensor(res[:, :, :], res[:, :, :],
                                           g_all[:, :].unsqueeze(1).to_broadcast([P, TB, D]),
                                           ALU.mult).then_inc(s["ln2_g"], 1)
                    if mid and n == 10:
                        rsqrt(mv3[:, :, 1], rs3, "ln3_mv", "ln3_ve", "ln3_rs", t)

            steps(pool, step)

        @block.scalar
        def _(act):
            act.wait_ge(s["w_loaded"], 16 * 15)
            act.activation(one_e[:, 0, 0:KH * NS],
                           a_neg[:, :, :].rearrange("p k n -> p (k n)"), ACT.Exp).then_inc(s["a_exped"], 1)

            def norm(dst, src, rs, nm, done):
                for j in range(TB):
                    last = act.activation(dst[:, j, :], src[:, j, :], ACT.Identity,
                                          scale=rs[:, j:j + 1], bias=nm[:, j:j + 1])
                last.then_inc(s[done], 1)

            def exps(t, par, n):
                if n == 0:
                    need(act, s["delta_done"], t + 1)
                for h in range(KH):
                    need(act, s["scan_done"], KH * NS * t + KH * n + h - DA_BANKS + 1)
                    act.activation(da_ps[:, (KH * n + h) % DA_BANKS, :], delta[:, par, h, :], ACT.Exp,
                                   scale=a_neg[:, h, n:n + 1]).then_inc(s["da_ready"], 1)

            def step(t, par, pre=False, scan=False, mid=False, end=False):
                nxt = 1 - par
                for n in range(NS):
                    if scan:
                        exps(t, par, n)
                    if end and n == 2:
                        for m in range(KH):
                            need(act, s["post_ready"], post_count(t, f"k{m}"))
                            act.activation(kact[:, m, :], post_ps[:, :], ACT.Relu).then_inc(s["post_read"], 1)
                        need(act, s["post_read"], post_count(t, "k1"))
                        act.activation(kact[:, :, :], kact[:, :, :], ACT.Square).then_inc(s["kact_done"], 1)
                    if pre and n == 4:
                        need(act, s["ln1_nm"], t + 2)
                        need(act, s["res_done"], t)
                        norm(xn_tok[:, nxt, :, :], x_tok, rs1, nm1, "xn_done")
                    if pre and n == 5:
                        for k in range(KH):
                            need(act, s["pre_ready"], pre_count(t + 1, f"xnT{k}"))
                            act.activation(xnT[:, k, :], pre_ps[:, :], ACT.Copy).then_inc(s["pre_read"], 1)
                    if mid and n == 6:
                        need(act, s["ln2_nm"], t)
                        norm(res, res, rs2, nm2, "ln2_norm")
                    if pre and n == 7:
                        need(act, s["gated_done"], t)
                        for m in range(KH):
                            need(act, s["pre_ready"], pre_count(t + 1, f"x{m}"))
                            act.activation(xT[:, nxt, m, :], pre_ps[:, :], ACT.Copy).then_inc(s["pre_read"], 1)
                        for m in range(KH):
                            need(act, s["pre_ready"], pre_count(t + 1, f"z{m}"))
                            act.activation(zs[:, nxt, m, :], pre_ps[:, :], ACT.Silu).then_inc(s["pre_read"], 1)
                    if end and n == 8:
                        need(act, s["out_stored"], 16 * (t - 2))
                        for v in range(2):
                            need(act, s["post_ready"], post_count(t, f"r{v}"))
                            act.activation(r_out[:, 2 * v:2 * v + 2, :], post_tok, ACT.Sigmoid).then_inc(s["post_read"], 1)
                    if pre and n == 8:
                        need(act, s["pre_ready"], pre_count(t + 1, "bc"))
                        need(act, s["bc_stored"], 16 * (t + 1))
                        act.activation(bc_rows[:, :], pre_ps[0:2 * NS, :], ACT.Copy).then_inc(s["pre_read"], 1)
                        need(act, s["pre_read"], pre_count(t + 1, "bc"))
                        act.sem_inc(s["bc_rows_done"], 1)
                    if pre and n == 9:
                        for m in range(KH):
                            need(act, s["pre_ready"], pre_count(t + 1, f"dt{m}"))
                            act.activation(abs_v[:, m, :], pre_ps[:, :], ACT.Abs,
                                           bias=bdt[:, m:m + 1]).then_inc(s["abs_done"], 1)
                            act.activation(relu_v[:, m, :], pre_ps[:, :], ACT.Relu,
                                           bias=bdt[:, m:m + 1]).then_inc(s["pre_read"], 1)
                        need(act, s["abs_done"], KH * (t + 2))
                        act.activation(abs_v[:, :, :], abs_v[:, :, :], ACT.Exp, scale=-1.0).then_inc(s["exp_done"], 1)
                        need(act, s["exp_done"], t + 2)
                        act.activation(one_e[:, :, :], abs_v[:, :, :], ACT.Copy, bias=1.0)
                        act.activation(ln_v[:, :, :], abs_v[:, :, :], ACT.Ln, bias=1.0).then_inc(s["ln_done"], 1)
                    if mid and n == 11:
                        need(act, s["ln3_nm"], t)
                        norm(res, xres[:, nxt, :, :], rs3, nm3, "hn_done")
                    if mid and n == 13:
                        need(act, s["prev_done"], t)
                        for k in range(KH):
                            need(act, s["post_ready"], post_count(t, f"hT{k}"))
                            act.activation(hT[:, k, 1:LC + 1], post_ps[:, :], ACT.Copy).then_inc(s["post_read"], 1)
                        need(act, s["post_read"], post_count(t, "hT1"))
                        for k in range(KH):
                            act.activation(xr[:, k, :], hT[:, k, 0:LC], ACT.Copy, scale=omr[:, k:k + 1])
                            last = act.activation(xk[:, k, :], hT[:, k, 0:LC], ACT.Copy, scale=omk[:, k:k + 1])
                        last.then_inc(s["mixed_prev"], 1)

            steps(act, step)

        @block.vector
        def _(dve):
            dve.memset(notfirst[:, :], 1.0).then_inc(s["flags0"], 1)
            dve.wait_ge(s["flags0"], 1)
            dve.memset(notfirst[:, 0:NT:CPB], 0.0).then_inc(s["flags_done"], 1)
            dve.memset(carry[:, :, :], 0.0).then_inc(s["flags_done"], 1)
            dve.memset(hT[:, :, LC:LC + 1], 0.0).then_inc(s["flags_done"], 1)
            dve.wait_ge(s["a_exped"], 1)
            dve.tensor_scalar(a_neg[:, :, :].rearrange("p k n -> p (k n)"), one_e[:, 0, 0:KH * NS], -1.0, None,
                              ALU.mult).then_inc(s["const_done"], 1)
            dve.wait_ge(s["w_loaded"], 16 * 15)
            dve.tensor_scalar(omr[:, :], mur[:, :], -1.0, 1.0, ALU.mult, ALU.add).then_inc(s["const_done"], 1)
            dve.tensor_scalar(omk[:, :], muk[:, :], -1.0, 1.0, ALU.mult, ALU.add).then_inc(s["const_done"], 1)
            for n, dst in enumerate([wxT, w_rT, w_kT, w_vT, w_dtx]):
                dve.wait_ge(s["setup_pe"], n + 1)
                bank = (pre_ps, post_ps)[n % 2]
                dve.tensor_copy(dst if n == 0 else dst[:, :, :],
                                bank[:, :].rearrange("p (k n) -> p k n", k=KH)).then_inc(s["setup_ev"], 1)
            dve.wait_ge(s["flags_done"], 3)

            def stats(src, st, mv, stat_sem, mv_sem, count):
                for j in range(TB):
                    last = dve.bn_stats(st[:, j, :], src[:, j, :])
                last.then_inc(s[stat_sem], 1)
                need(dve, s[stat_sem], count)
                dve.sem_inc(s["dve_waited"], 1)
                for j in range(TB):
                    last = dve.bn_aggr(mv[:, j, :], st[:, j, :])
                last.then_inc(s[mv_sem], 1)

            def neg_mean(mv, rs, nm, rs_sem, nm_sem, count):
                need(dve, s[rs_sem], count)
                dve.scalar_tensor_tensor(nm[:, :], mv[:, :, 0], -1.0, rs[:, :], ALU.mult,
                                         ALU.mult).then_inc(s[nm_sem], 1)

            def times_b(t, par, n):
                if n % GN == VEC_COLS[0]:
                    need(dve, b_loaded[n // GN], 16 * (t + 1))
                if n == VEC_COLS[0]:
                    need(dve, s["u_done"], t + 1)
                need(dve, s["scan_done"], 2 * NS * t + KH * (n - RING + 1))
                dve.tensor_tensor(dbx[:, n % RING, :, :], u[:, par, :, :],
                                  b_ring[:, n // GN % BG, n % GN:n % GN + 1, :].to_broadcast([P, KH, LC]),
                                  ALU.mult).then_inc(s["dbx_vec"], 1)

            def keep_carry(t, n):
                need(dve, s["scan_done"], KH * NS * t + KH * (n + 1))
                dve.tensor_copy(carry[:, n, :], hg[:, n % RING, :, LC - 1]).then_inc(s["carry_saved"], 1)

            def step(t, par, pre=False, scan=False, mid=False, end=False):
                nxt = 1 - par
                if scan:
                    need(dve, s["carry_saved"], NS * t)
                    dve.tensor_scalar(carry[:, :, :].rearrange("p n k -> p (n k)"),
                                      carry[:, :, :].rearrange("p n k -> p (n k)"),
                                      notfirst[:, bass.ds(t, 1)], None, ALU.mult).then_inc(s["carry_in"], 1)
                    times_b(t, par, 0)
                    need(dve, s["carry_in"], t + 1)
                for n in range(NS):
                    if scan:
                        if n + 1 in VEC_COLS:
                            times_b(t, par, n + 1)
                        if n in VEC_COLS:
                            need(dve, s["dbx_vec"], len(VEC_COLS) * t + made(VEC_COLS, n))
                        else:
                            need(dve, s["dbx_pool"], len(POOL_COLS) * t + made(POOL_COLS, n))
                        need(dve, s["y_added"], NS * t + n - RING + 1)
                        for h in range(KH):
                            need(dve, s["da_ready"], KH * NS * t + KH * n + h + 1)
                            dve.tensor_tensor_scan(hg[:, n % RING, h, :], da_ps[:, (KH * n + h) % DA_BANKS, :],
                                                   dbx[:, n % RING, h, :], carry[:, n, h:h + 1],
                                                   ALU.mult, ALU.add).then_inc(s["scan_done"], 1)
                        if n >= 1:
                            keep_carry(t, n - 1)
                    if mid and n == 1:
                        need(dve, s["y_added"], NS * t)
                        for h in range(KH):
                            last = dve.scalar_tensor_tensor(gated[:, h, :], xT[:, nxt, h, :], d_par[:, h:h + 1],
                                                            y_ps[:, h, :], ALU.mult, ALU.add)
                        last.then_inc(s["y_read"], 1)
                        need(dve, s["y_read"], t)
                        dve.tensor_tensor(gated[:, :, :], gated[:, :, :], zs[:, nxt, :, :],
                                          ALU.mult).then_inc(s["gated_done"], 1)
                    if pre and n == 1:
                        need(dve, s["x_loaded"], 16 * (t + 2))
                        stats(x_tok, st1, mv1, "ln1_stat", "ln1_mv", t + 2)
                    if pre and n == 3:
                        neg_mean(mv1, rs1, nm1, "ln1_rs", "ln1_nm", t + 2)
                    if mid and n == 4:
                        for v in range(2):
                            need(dve, s["post_ready"], post_count(t, f"wo{v}"))
                            dve.tensor_tensor(res[:, 2 * v:2 * v + 2, :], post_tok,
                                              xn_tok[:, nxt, 2 * v:2 * v + 2, :], ALU.add).then_inc(s["post_read"], 1)
                        need(dve, s["post_read"], post_count(t, "wo1"))
                        dve.sem_inc(s["res_done"], 1)
                        stats(res, st2, mv2, "ln2_stat", "ln2_mv", t)
                    if mid and n == 6:
                        neg_mean(mv2, rs2, nm2, "ln2_rs", "ln2_nm", t)
                    if mid and n == 8:
                        need(dve, s["ln2_g"], t)
                        dve.tensor_tensor(res[:, :, :], res[:, :, :], b_all[:, :].unsqueeze(1).to_broadcast([P, TB, D]),
                                          ALU.add).then_inc(s["ln2_b"], 1)
                        need(dve, s["xres_loaded"], 16 * t)
                        need(dve, s["ln2_b"], t)
                        dve.tensor_tensor(xres[:, nxt, :, :], xres[:, nxt, :, :], res[:, :, :],
                                          ALU.add).then_inc(s["x2_done"], 1)
                    if mid and n == 9:
                        need(dve, s["x2_done"], t)
                        stats(xres[:, nxt, :, :], st3, mv3, "ln3_stat", "ln3_mv", t)
                    if mid and n == 10:
                        pass
                    if mid and n == 11:
                        neg_mean(mv3, rs3, nm3, "ln3_rs", "ln3_nm", t)
                    if end and n == 11:
                        need(dve, s["post_ready"], post_count(t, "v0"))
                        for v in range(2):
                            need(dve, s["post_ready"], post_count(t, f"v{v}"))
                            dve.tensor_tensor(r_out[:, 2 * v:2 * v + 2, :], r_out[:, 2 * v:2 * v + 2, :], post_tok,
                                              ALU.mult).then_inc(s["post_read"], 1)
                        need(dve, s["post_read"], post_count(t, "v1"))
                        dve.tensor_tensor(r_out[:, :, :], r_out[:, :, :], xres[:, par, :, :],
                                          ALU.add).then_inc(s["ffn_done"], 1)
                    if pre and n == 12:
                        need(dve, s["ln_done"], t + 2)
                        dve.scalar_tensor_tensor(one_e[:, :, :].rearrange("p k l -> p (k l)"),
                                                 one_e[:, :, :].rearrange("p k l -> p (k l)"), 1.0,
                                                 abs_v[:, :, :].rearrange("p k l -> p (k l)"),
                                                 ALU.subtract, ALU.subtract).then_inc(s["nc_done"], 1)
                        need(dve, s["nc_done"], t + 2)
                        dve.tensor_tensor(relu_v[:, :, :], relu_v[:, :, :], one_e[:, :, :],
                                          ALU.subtract).then_inc(s["rl_done"], 1)
                        need(dve, s["rl_done"], t + 2)
                        dve.tensor_tensor(delta[:, nxt, :, :], relu_v[:, :, :], ln_v[:, :, :],
                                          ALU.add).then_inc(s["delta_done"], 1)
                    if mid and n == 12:
                        need(dve, s["mixed"], t - 1)
                        dve.tensor_scalar(hT[:, :, 0], hT[:, :, LC], notfirst[:, bass.ds(t - 1, 1)], None,
                                          ALU.mult).then_inc(s["prev_done"], 1)
                    if pre and n == 13:
                        need(dve, s["delta_done"], t + 2)
                        dve.tensor_tensor(u[:, nxt, :, :], delta[:, nxt, :, :], xT[:, nxt, :, :],
                                          ALU.mult).then_inc(s["u_done"], 1)
                    if mid and n == 15:
                        need(dve, s["mixed_prev"], t)
                        for mix, mu in ((xk, muk), (xr, mur)):
                            for k in range(KH):
                                last = dve.scalar_tensor_tensor(mix[:, k, :], hT[:, k, 1:LC + 1], mu[:, k:k + 1],
                                                                mix[:, k, :], ALU.mult, ALU.add)
                        last.then_inc(s["mixed"], 1)
                if scan:
                    keep_carry(t, NS - 1)

            steps(dve, step)

        @block.tensor
        def _(pe):
            pe.wait_ge(s["ident_done"], 1)
            pe.wait_ge(s["w_loaded"], 16 * 15)
            for n, src in enumerate([wx_raw] + raw):
                bank = (pre_ps, post_ps)[n % 2]
                if n >= 2:
                    pe.wait_ge(s["setup_ev"], n - 1)
                for k in range(KH):
                    for m in range(KH):
                        last = pe.transpose(bank[:, m * D + k * P:m * D + k * P + P], src[:, k, m * P:(m + 1) * P],
                                            ident[:, :])
                last.then_inc(s["setup_pe"], 1)
            pe.wait_ge(s["setup_ev"], 3)
            for m in range(KH):
                for k in range(KH):
                    last = pe.matmul(pre_ps[:, m * D:(m + 1) * D], wxT[:, k, m * P:(m + 1) * P], wdt_raw[:, k, :],
                                     start=k == 0, stop=k == KH - 1)
            last.then_inc(s["setup_pe"], 1)
            pe.wait_ge(s["setup_ev"], 5)

            def add_up(t, n):
                need(pe, s["g_ready"], NS * t + n + 1)
                if n == 0:
                    need(pe, s["y_read"], t)
                for h in range(KH):
                    last = pe.matmul(y_ps[:, h, :], ident[:, :], hg[:, n % RING, h, :], start=n == 0, stop=n == NS - 1)
                last.then_inc(s["y_added"], 1)

            def project(out, w, x, cols):
                for k in range(KH):
                    last = pe.matmul(out, w[:, k, cols], x[:, k, :], start=k == 0, stop=k == KH - 1)
                return last

            def by_token(v, xT_, w):
                for b in range(2):
                    for k in range(KH):
                        last = pe.matmul(post_tok[:, b, :], xT_[:, k, (2 * v + b) * P:(2 * v + b + 1) * P], w[:, k, :],
                                         start=k == 0, stop=k == KH - 1)
                return last

            def turned(bank, src, k):
                for j in range(TB):
                    last = pe.transpose(bank[:, j * P:(j + 1) * P], src[:, j, k * P:(k + 1) * P], ident[:, :])
                return last

            def step(t, par, pre=False, scan=False, mid=False, end=False):
                nxt = 1 - par
                i = t + 1

                def pre_unit(unit):
                    need(pe, s["pre_read"], pre_count(i, unit) - 1)
                    m = int(unit[-1]) if unit != "bc" else 0
                    cols = slice(m * P, (m + 1) * P)
                    if unit in ("xnT0", "xnT1"):
                        need(pe, s["xn_done"], i + 1)
                        last = turned(pre_ps, xn_tok[:, nxt, :, :], m)
                    elif unit in ("x0", "x1"):
                        need(pe, s["pre_read"], pre_count(i, "xnT1"))
                        last = project(pre_ps[:, :], w_in, xnT, cols)
                    elif unit in ("z0", "z1"):
                        last = project(pre_ps[:, :], w_in, xnT, slice(D + m * P, D + (m + 1) * P))
                    elif unit == "bc":
                        last = project(pre_ps[0:2 * NS, :], w_bc, xT[:, nxt, :, :], slice(0, 2 * NS))
                    else:
                        last = project(pre_ps[:, :], w_dtx, xT[:, nxt, :, :], cols)
                    last.then_inc(s["pre_ready"], 1)

                def post_unit(unit):
                    need(pe, s["post_read"], post_count(t, unit) - 1)
                    m = int(unit[-1])
                    cols = slice(m * P, (m + 1) * P)
                    if unit[:2] == "wo":
                        need(pe, s["gated_done"], t)
                        last = by_token(m, gated, w_out)
                    elif unit[:2] == "hT":
                        need(pe, s["hn_done"], t)
                        last = turned(post_ps, res, m)
                    elif unit[0] == "k":
                        need(pe, s["mixed"], t - 1)
                        last = project(post_ps[:, :], w_kT, xk, cols)
                    elif unit[0] == "r":
                        last = by_token(m, xr, w_rT)
                    else:
                        need(pe, s["kact_done"], t - 1)
                        last = by_token(m, kact, w_vT)
                    last.then_inc(s["post_ready"], 1)

                at = {0: ["k0"], 1: ["k1"], 2: ["wo0"], 3: ["wo1"], 5: ["xnT0", "xnT1"], 6: ["x0", "x1"],
                      7: ["z0", "z1", "r0"], 8: ["r1", "bc"], 9: ["dt0", "dt1"], 10: ["v0"], 11: ["v1"],
                      12: ["hT0"], 13: ["hT1"]}
                for n in range(NS):
                    if scan and n >= 1:
                        add_up(t, n - 1)
                    for unit in at.get(n, ()):
                        if unit in PRE and pre:
                            pre_unit(unit)
                        if (unit in POST_A and mid) or (unit in POST_B and end):
                            post_unit(unit)
                if scan:
                    add_up(t, NS - 1)

            steps(pe, step)


_INS = ["L0_attn_x_in", "L0_attn_W_in", "L0_attn_W_x", "L0_attn_W_dt", "L0_attn_b_dt", "L0_attn_A_log",
        "L0_attn_D_param", "L0_attn_W_out", "L0_attn_ln_g", "L0_attn_ln_b", "L0_ffn_W_r", "L0_ffn_W_k",
        "L0_ffn_W_v", "L0_ffn_mu_r", "L0_ffn_mu_k"]
_OUT = ((BATCH, LEN, D), "float32")


def kernel(**inputs):
    import numpy as _np
    import concourse.bacc as _bacc
    from concourse import mybir as _mybir
    from concourse.bass_utils import run_bass_kernel_spmd as _run

    nc = _bacc.Bacc("TRN2", target_bir_lowering=False, num_devices=1)
    arrays, args = {}, []
    for name in _INS:
        a = _np.ascontiguousarray(inputs[name])
        arrays[f"in_{name}_dram"] = a
        args.append(nc.dram_tensor(f"in_{name}_dram", a.shape, _mybir.dt.from_np(a.dtype), kind="ExternalInput").ap())
    shape, dtype = _OUT
    args.append(nc.dram_tensor("out_0_dram", shape, _mybir.dt.from_np(_np.dtype(dtype)), kind="ExternalOutput").ap())
    mamba_rwkv_layer(nc, *args)
    r = _run(nc, [arrays], core_ids=[0])
    return r.results[0]["out_0_dram"]
```

```python
from contextlib import ExitStack

import concourse.bass as bass
from concourse import mybir

P = 128
BATCH, LEN, D = 4, 2048, 256
NS = 16
LC = 512
TB = LC // P
KH = D // P
CPB = LEN // LC
NT = BATCH * CPB
EPS = 1e-5
GN = 4
GROUPS = NS // GN
BG = 2
X_RING = 4
H_RING = 8
DA_BANKS = 4
B_LEAD, C_LAG, Y_LAG = 2, 2, 4

F32 = mybir.dt.float32
ALU = mybir.AluOpType
ACT = mybir.ActivationFunctionType

POOL_COLS = [n for n in range(NS) if n % 2 == 1]
VEC_COLS = [n for n in range(NS) if n % 2 == 0]


def made(cols, n):
    return sum(c <= n for c in cols)


def need(eng, sem, count):
    if not (isinstance(count, int) and count <= 0):
        eng.wait_ge(sem, count)


def mamba_rwkv_layer(nc, x_in, W_in, W_x, W_dt, b_dt, A_log, D_param, W_out, ln_g, ln_b,
                     W_r, W_k, W_v, mu_r, mu_k, out):
    x_v = x_in.rearrange("b (c j p) d -> (b c) p j d", p=P, j=TB)
    out_v = out.rearrange("b (c j p) d -> (b c) p j d", p=P, j=TB)
    bc_dram = nc.dram_tensor("bc_rows_dram", (NT, 2 * NS, LC), F32).ap()

    def halves(w):
        return w.rearrange("(k p) n -> p k n", p=P)

    def column(v):
        return v.rearrange("(k p) -> p k", p=P)

    with ExitStack() as ctx:
        def sb(name, *shape):
            return ctx.enter_context(nc.sbuf_tensor(name, list(shape), F32))

        def ps(name, *shape):
            return ctx.enter_context(nc.psum_tensor(name, list(shape), F32))

        def sem(name):
            return ctx.enter_context(nc.semaphore(name))

        ident = sb("ident", P, P)
        w_in = sb("w_in", P, KH, 2 * D)
        w_bc = sb("w_bc", P, KH, 2 * NS)
        w_dtx = sb("w_dtx", P, KH, D)
        w_out = sb("w_out", P, KH, D)
        w_rT = sb("w_rT", P, KH, D)
        w_kT = sb("w_kT", P, KH, D)
        w_vT = sb("w_vT", P, KH, D)
        bdt = sb("bdt", P, KH)
        a_neg = sb("a_neg", P, KH, NS)
        d_par = sb("d_par", P, KH)
        mur = sb("mur", P, KH)
        muk = sb("muk", P, KH)
        omr = sb("omr", P, KH)
        omk = sb("omk", P, KH)
        g_all = sb("g_all", P, D)
        b_all = sb("b_all", P, D)
        notfirst = sb("notfirst", P, NT)
        neg_half = sb("neg_half", P, TB)
        eps_tile = sb("eps_tile", P, TB)
        ln_of_1 = sb("ln_of_1", P, 1)
        x_tok = sb("x_tok", P, TB, D)
        xn_tok = sb("xn_tok", P, 2, TB, D)
        xnT = sb("xnT", P, KH, LC)
        xT = sb("xT", P, 2, KH, LC)
        zs = sb("zs", P, 2, KH, LC)
        bc_rows = sb("bc_rows", 2 * NS, LC)
        relu_v = sb("relu_v", P, KH, LC)
        ln_v = sb("ln_v", P, KH, LC)
        one_e = sb("one_e", P, KH, LC)
        abs_v = sb("abs_v", P, KH, LC)
        delta = sb("delta", P, 2, KH, LC)
        u = sb("u", P, 2, KH, LC)
        st1 = sb("st1", P, TB, 6)
        mv1 = sb("mv1", P, TB, 2)
        rs1 = sb("rs1", P, TB)
        nm1 = sb("nm1", P, TB)
        b_ring = sb("b_ring", P, BG, GN, LC)
        c_ring = sb("c_ring", P, BG, GN, LC)
        dbx = sb("dbx", P, X_RING, KH, LC)
        hg = sb("hg", P, H_RING, KH, LC)
        carry = sb("carry", P, NS, KH)
        keep = sb("keep", P, 2)
        xres = sb("xres", P, 2, TB, D)
        gated = sb("gated", P, KH, LC)
        res = sb("res", P, TB, D)
        st2 = sb("st2", P, TB, 6)
        mv2 = sb("mv2", P, TB, 2)
        rs2 = sb("rs2", P, TB)
        st3 = sb("st3", P, TB, 6)
        mv3 = sb("mv3", P, TB, 2)
        rs3 = sb("rs3", P, TB)
        nm3 = sb("nm3", P, TB)
        hT = sb("hT", P, KH, LC + 1)
        xr = sb("xr", P, KH, LC)
        xk = sb("xk", P, KH, LC)
        kact = sb("kact", P, KH, LC)
        r_out = sb("r_out", P, TB, D)
        wx_raw = c_ring[:, 0, 0:1, :].rearrange("p a (k n) -> p (a k) n", k=KH)
        wdt_raw = c_ring[:, 0, 1:2, :].rearrange("p a (k n) -> p (a k) n", k=KH)
        wxT = c_ring[:, 0, 2:3, :].rearrange("p a (k n) -> p (a k) n", k=KH)
        raw = [b_ring[:, 0, m:m + 1, :].rearrange("p a (k n) -> p (a k) n", k=KH) for m in range(3)]

        y_ps = ps("y_ps", P, KH, LC)
        da_ps = ps("da_ps", P, DA_BANKS, LC)
        pre_ps = ps("pre_ps", P, LC)
        post_ps = ps("post_ps", P, LC)
        post_tok = post_ps[:, :].rearrange("p (s d) -> p s d", d=D)

        names = """w_loaded ident0 ident_done flags0 flags_done half_done a_exped const_done
            dve_waited sp_waited setup_pe setup_ev ln1_done
            x_loaded xres_loaded bc_stored out_stored
            ln1_stat ln1_mv ln1_ve ln1_rs ln1_nm xn_done pre_ready pre_read bc_rows_done
            abs_done exp_done ln_done nc_done rl_done delta_done u_done
            keep_set scan_done carry_saved da_ready dbx_vec dbx_pool g_ready y_added
            y_read gated_done z_done post_ready post_read res_set xb_done
            ln2_stat ln2_mv ln2_ve ln2_rs ln2_g x2_done
            ln3_stat ln3_mv ln3_ve ln3_rs ln3_nm hn_done prev_done mixed_prev mixed
            kact_done sig_done ffn_done""".split()
        s = {name: sem(name) for name in names}
        b_loaded = [sem(f"b_loaded{g}") for g in range(GROUPS)]
        c_loaded = [sem(f"c_loaded{g}") for g in range(GROUPS)]
        block = ctx.enter_context(nc.Block())

        PRE = ["xnT0", "xnT1", "x0", "x1", "bc", "dt0", "dt1", "z0", "z1"]
        POST = ["k0", "k1", "r0", "r1", "wo0", "wo1", "v0", "v1", "hT0", "hT1"]
        POST_A = ["wo0", "wo1", "hT0", "hT1"]
        POST_B = ["k0", "k1", "r0", "r1", "v0", "v1"]

        def pre_count(i, unit):
            return len(PRE) * i + PRE.index(unit) + 1

        def post_count(t, unit):
            if isinstance(t, int) and t == 1:
                return POST_A.index(unit) + 1
            if isinstance(t, int) and t == NT + 1:
                return len(POST_A) + len(POST) * (NT - 1) + POST_B.index(unit) + 1
            return len(POST) * (t - 2) + len(POST_A) + POST.index(unit) + 1

        def steps(eng, step):
            step(-1, 1, pre=True)
            step(0, 0, pre=True, scan=True)
            step(1, 1, pre=True, scan=True, mid=True)
            with eng.Fori(0, (NT - 4) // 2) as pair:
                step(2 * pair + 2, 0, pre=True, scan=True, mid=True, end=True)
                step(2 * pair + 3, 1, pre=True, scan=True, mid=True, end=True)
            step(NT - 2, 0, pre=True, scan=True, mid=True, end=True)
            step(NT - 1, 1, scan=True, mid=True, end=True)
            step(NT, 0, mid=True, end=True)
            step(NT + 1, 1, end=True)

        def column_at(t, par, n, scan, pre, mid):
            if n >= NS:
                return (t + 1, 1 - par, n - NS) if pre else None
            if n < 0:
                return (t - 1, 1 - par, n + NS) if mid else None
            return (t, par, n) if scan else None

        def b_of(n):
            return b_ring[:, n // GN % BG, n % GN:n % GN + 1, :].to_broadcast([P, KH, LC])

        def c_of(n):
            return c_ring[:, n // GN % BG, n % GN:n % GN + 1, :].to_broadcast([P, KH, LC])

        @block.sync
        def _(sp):
            loads = [(w_in[:, :, :], halves(W_in)),
                     (w_bc[:, :, :], halves(W_x)[:, :, D:]),
                     (wx_raw, halves(W_x)[:, :, 0:D]),
                     (wdt_raw, halves(W_dt)),
                     (w_out[:, :, :], halves(W_out)),
                     (raw[0], halves(W_r)), (raw[1], halves(W_k)), (raw[2], halves(W_v)),
                     (a_neg[:, :, :], halves(A_log))]
            loads += [(dst[:, :], v.rearrange("(o d) -> o d", o=1).partition_broadcast(P))
                      for dst, v in ((g_all, ln_g), (b_all, ln_b))]
            sp.dma_start(x_tok[:, :, :], x_v[0]).then_inc(s["x_loaded"], 16)
            for dst, src in loads:
                sp.dma_start(dst, src).then_inc(s["w_loaded"], 16)
            for dst, v in ((bdt, b_dt), (d_par, D_param), (mur, mu_r), (muk, mu_k)):
                sp.dma_start(dst[:, :], column(v), allow_slow_non_contiguous=True).then_inc(s["w_loaded"], 16)

            def arrived(sem, count):
                need(sp, sem, count)
                sp.sem_inc(s["sp_waited"], 1)

            def slot_before(i, g):
                return (i, g - BG) if g >= BG else (i - 1, g + BG)

            def load_b(i, g, first=False):
                if not first:
                    before, at = slot_before(i, g)
                    last = GN * at + GN - 1
                    arrived(s["dbx_vec"], len(VEC_COLS) * before + made(VEC_COLS, last))
                    arrived(s["dbx_pool"], len(POOL_COLS) * before + made(POOL_COLS, last))
                sp.dma_start(b_ring[:, g % BG, :, :],
                             bc_dram[i, GN * g:GN * g + GN, :].partition_broadcast(P)).then_inc(b_loaded[g], 16)

            def load_c(i, g, first=False):
                if not first:
                    before, at = slot_before(i, g)
                    arrived(s["g_ready"], NS * before + GN * at + GN)
                sp.dma_start(c_ring[:, g % BG, :, :],
                             bc_dram[i, NS + GN * g:NS + GN * g + GN, :].partition_broadcast(P)).then_inc(c_loaded[g], 16)

            def step(t, par, pre=False, scan=False, mid=False, end=False):
                start = isinstance(t, int) and t == -1
                if mid:
                    arrived(s["ffn_done"], t - 2)
                    arrived(s["x2_done"], t - 1)
                    sp.dma_start(xres[:, 1 - par, :, :], x_v[t - 1]).then_inc(s["xres_loaded"], 16)
                if scan:
                    if not (isinstance(t, int) and t == 0):
                        load_c(t, 1)
                if pre and not (isinstance(t, int) and t == NT - 2):
                    arrived(s["xn_done"], t + 2)
                    sp.dma_start(x_tok[:, :, :], x_v[t + 2]).then_inc(s["x_loaded"], 16)
                if scan:
                    load_b(t, 2)
                    load_c(t, 2)
                    load_b(t, 3)
                if pre:
                    arrived(s["bc_rows_done"], t + 2)
                    sp.dma_start(bc_dram[t + 1], bc_rows[:, :]).then_inc(s["bc_stored"], 16)
                if end:
                    arrived(s["ffn_done"], t - 1)
                    sp.dma_start(out_v[t - 2], r_out[:, :, :]).then_inc(s["out_stored"], 16)
                if scan:
                    load_c(t, 3)
                if pre:
                    arrived(s["bc_stored"], 16 * (t + 2))
                    if start:
                        arrived(s["setup_ev"], 5)
                    load_b(t + 1, 0, start)
                    load_c(t + 1, 0, start)
                    load_b(t + 1, 1, start)
                    if start:
                        load_c(0, 1, True)

            steps(sp, step)
            sp.wait_ge(s["out_stored"], 16 * NT)

        @block.gpsimd
        def _(pool):
            pool.memset(ident[:, :], 0.0).then_inc(s["ident0"], 1)
            pool.wait_ge(s["ident0"], 1)
            pool.affine_select(out=ident[:, :], in_=ident[:, :], compare_op=ALU.not_equal, fill=1.0, base=0,
                               pattern=[[-1, P]], channel_multiplier=1).then_inc(s["ident_done"], 1)

            pool.memset(eps_tile[:, :], EPS).then_inc(s["half_done"], 1)
            pool.memset(neg_half[:, :], -0.5).then_inc(s["half_done"], 1)
            pool.wait_ge(s["half_done"], 2)

            def rsqrt(var, rs, mv_sem, ve_sem, rs_sem, count):
                need(pool, s[mv_sem], count)
                pool.tensor_tensor(rs[:, :], var, eps_tile[:, :], ALU.add).then_inc(s[ve_sem], 1)
                need(pool, s[ve_sem], count)
                pool.tensor_tensor(rs[:, :], rs[:, :], neg_half[:, :], ALU.pow).then_inc(s[rs_sem], 1)

            def times_b(i, ip, n):
                need(pool, b_loaded[n // GN], 16 * (i + 1))
                need(pool, s["u_done"], i + 1)
                need(pool, s["scan_done"], KH * (NS * i + n - X_RING + 1))
                pool.tensor_tensor(dbx[:, n % X_RING, :, :], u[:, ip, :, :], b_of(n),
                                   ALU.mult).then_inc(s["dbx_pool"], 1)

            def times_c(i, n):
                need(pool, c_loaded[n // GN], 16 * (i + 1))
                need(pool, s["carry_saved"], NS * i + n + 1)
                pool.tensor_tensor(hg[:, n % H_RING, :, :], hg[:, n % H_RING, :, :], c_of(n),
                                   ALU.mult).then_inc(s["g_ready"], 1)

            def step(t, par, pre=False, scan=False, mid=False, end=False):
                nxt = 1 - par
                for n in range(NS):
                    ahead = column_at(t, par, n + B_LEAD, scan, pre, mid)
                    if ahead and ahead[2] in POOL_COLS:
                        times_b(*ahead)
                    behind = column_at(t, par, n - C_LAG, scan, pre, mid)
                    if behind:
                        times_c(behind[0], behind[2])
                    if pre and n == 1:
                        rsqrt(mv1[:, :, 1], rs1, "ln1_mv", "ln1_ve", "ln1_rs", t + 2)
                    if mid and n == 5:
                        need(pool, s["xres_loaded"], 16 * t)
                        pool.tensor_tensor(xres[:, nxt, :, :], xres[:, nxt, :, :],
                                           b_all[:, :].unsqueeze(1).to_broadcast([P, TB, D]),
                                           ALU.add).then_inc(s["xb_done"], 1)
                    if mid and n == 8:
                        rsqrt(mv2[:, :, 1], rs2, "ln2_mv", "ln2_ve", "ln2_rs", t)
                    if mid and n == 10:
                        rsqrt(mv3[:, :, 1], rs3, "ln3_mv", "ln3_ve", "ln3_rs", t)

            steps(pool, step)

        @block.scalar
        def _(act):
            act.wait_ge(s["w_loaded"], 16 * 15)
            act.activation(one_e[:, 0, 0:KH * NS], a_neg[:, :, :].rearrange("p k n -> p (k n)"),
                           ACT.Exp).then_inc(s["a_exped"], 1)
            act.wait_ge(s["half_done"], 2)
            act.activation(ln_of_1[:, :], eps_tile[:, 0:1], ACT.Ln, scale=0.0, bias=1.0).then_inc(s["ln1_done"], 1)

            def norm(dst, src, rs, nm, done):
                for j in range(TB):
                    last = act.activation(dst[:, j, :], src[:, j, :], ACT.Identity,
                                          scale=rs[:, j:j + 1], bias=nm[:, j:j + 1])
                last.then_inc(s[done], 1)

            def exps(i, ip, n):
                need(act, s["delta_done"], i + 1)
                for h in range(KH):
                    need(act, s["scan_done"], KH * (NS * i + n) + h - DA_BANKS + 1)
                    act.activation(da_ps[:, (KH * n + h) % DA_BANKS, :], delta[:, ip, h, :], ACT.Exp,
                                   scale=a_neg[:, h, n:n + 1]).then_inc(s["da_ready"], 1)

            def step(t, par, pre=False, scan=False, mid=False, end=False):
                nxt = 1 - par

                def from_pre(unit, dst):
                    need(act, s["pre_ready"], pre_count(t + 1, unit))
                    act.activation(dst, pre_ps[:, :], ACT.Copy).then_inc(s["pre_read"], 1)

                def relu_k(m):
                    need(act, s["post_ready"], post_count(t, f"k{m}"))
                    act.activation(kact[:, m, :], post_ps[:, :], ACT.Relu).then_inc(s["post_read"], 1)

                def raw_r(v):
                    need(act, s["out_stored"], 16 * (t - 2))
                    need(act, s["post_ready"], post_count(t, f"r{v}"))
                    act.activation(r_out[:, 2 * v:2 * v + 2, :], post_tok, ACT.Copy).then_inc(s["post_read"], 1)

                def softplus_in(m):
                    need(act, s["pre_ready"], pre_count(t + 1, f"dt{m}"))
                    act.activation(abs_v[:, m, :], pre_ps[:, :], ACT.Abs, bias=bdt[:, m:m + 1]).then_inc(s["abs_done"], 1)
                    act.activation(relu_v[:, m, :], pre_ps[:, :], ACT.Relu, bias=bdt[:, m:m + 1]).then_inc(s["pre_read"], 1)

                for n in range(NS):
                    ahead = column_at(t, par, n + 1, scan, pre, mid)
                    if ahead:
                        exps(*ahead)
                    if end and n == 1:
                        relu_k(0)
                    if mid and n == 1:
                        need(act, s["post_ready"], post_count(t - 1, "hT1") if not isinstance(t, int) or t > 1 else 0)
                        act.activation(res[:, :, :], xn_tok[:, nxt, :, :], ACT.Copy).then_inc(s["res_set"], 1)
                    if end and n == 2:
                        relu_k(1)
                        need(act, s["post_read"], post_count(t, "k1"))
                        act.activation(kact[:, :, :], kact[:, :, :], ACT.Square).then_inc(s["kact_done"], 1)
                    if pre and n == 2:
                        need(act, s["ln1_nm"], t + 2)
                        need(act, s["res_set"], t)
                        norm(xn_tok[:, nxt, :, :], x_tok, rs1, nm1, "xn_done")
                    if end and n == 3:
                        raw_r(0)
                    if pre and n in (4, 5):
                        from_pre(f"xnT{n - 4}", xnT[:, n - 4, :])
                    if end and n == 4:
                        raw_r(1)
                        need(act, s["post_read"], post_count(t, "r1"))
                        act.activation(r_out[:, :, :], r_out[:, :, :], ACT.Sigmoid).then_inc(s["sig_done"], 1)
                    if scan and n == 4:
                        need(act, s["pre_read"], pre_count(t, "z1"))
                        act.activation(zs[:, par, :, :], zs[:, par, :, :], ACT.Silu).then_inc(s["z_done"], 1)
                    if pre and n in (7, 8):
                        need(act, s["gated_done"], t)
                        from_pre(f"x{n - 7}", xT[:, nxt, n - 7, :])
                    if pre and n == 9:
                        need(act, s["pre_ready"], pre_count(t + 1, "bc"))
                        need(act, s["bc_stored"], 16 * (t + 1))
                        act.activation(bc_rows[:, :], pre_ps[0:2 * NS, :], ACT.Copy).then_inc(s["pre_read"], 1)
                        need(act, s["pre_read"], pre_count(t + 1, "bc"))
                        act.sem_inc(s["bc_rows_done"], 1)
                    if pre and n == 10:
                        softplus_in(0)
                    if pre and n == 11:
                        softplus_in(1)
                        need(act, s["abs_done"], KH * (t + 2))
                        act.activation(abs_v[:, :, :], abs_v[:, :, :], ACT.Exp, scale=-1.0).then_inc(s["exp_done"], 1)
                        need(act, s["exp_done"], t + 2)
                        act.activation(one_e[:, :, :], abs_v[:, :, :], ACT.Copy, bias=1.0)
                        act.activation(ln_v[:, :, :], abs_v[:, :, :], ACT.Ln, bias=1.0).then_inc(s["ln_done"], 1)
                    if mid and n == 11:
                        need(act, s["ln3_nm"], t)
                        norm(res, xres[:, nxt, :, :], rs3, nm3, "hn_done")
                    if pre and n in (12, 13):
                        from_pre(f"z{n - 12}", zs[:, nxt, n - 12, :])
                    if mid and n in (13, 14):
                        k = n - 13
                        need(act, s["prev_done"], t)
                        need(act, s["post_ready"], post_count(t, f"hT{k}"))
                        act.activation(hT[:, k, 1:LC + 1], post_ps[:, :], ACT.Copy).then_inc(s["post_read"], 1)
                    if mid and n == 14:
                        need(act, s["post_read"], post_count(t, "hT1"))
                        for k in range(KH):
                            act.activation(xr[:, k, :], hT[:, k, 0:LC], ACT.Copy, scale=omr[:, k:k + 1])
                            last = act.activation(xk[:, k, :], hT[:, k, 0:LC], ACT.Copy, scale=omk[:, k:k + 1])
                        last.then_inc(s["mixed_prev"], 1)

            steps(act, step)

        @block.vector
        def _(dve):
            dve.memset(notfirst[:, :], 1.0).then_inc(s["flags0"], 1)
            dve.wait_ge(s["flags0"], 1)
            dve.memset(notfirst[:, 0:NT:CPB], 0.0).then_inc(s["flags_done"], 1)
            dve.memset(carry[:, :, :], 0.0).then_inc(s["flags_done"], 1)
            dve.memset(hT[:, :, LC:LC + 1], 0.0).then_inc(s["flags_done"], 1)
            dve.wait_ge(s["a_exped"], 1)
            dve.tensor_scalar(a_neg[:, :, :].rearrange("p k n -> p (k n)"), one_e[:, 0, 0:KH * NS], -1.0, None,
                              ALU.mult).then_inc(s["const_done"], 1)
            dve.wait_ge(s["w_loaded"], 16 * 15)
            dve.tensor_scalar(omr[:, :], mur[:, :], -1.0, 1.0, ALU.mult, ALU.add).then_inc(s["const_done"], 1)
            dve.tensor_scalar(omk[:, :], muk[:, :], -1.0, 1.0, ALU.mult, ALU.add).then_inc(s["const_done"], 1)
            for n, dst in enumerate([wxT, w_rT, w_kT, w_vT, w_dtx]):
                dve.wait_ge(s["setup_pe"], n + 1)
                bank = (pre_ps, post_ps)[n % 2]
                dve.tensor_copy(dst if n == 0 else dst[:, :, :],
                                bank[:, :].rearrange("p (k n) -> p k n", k=KH)).then_inc(s["setup_ev"], 1)
            dve.wait_ge(s["flags_done"], 3)
            dve.wait_ge(s["ln1_done"], 1)

            def stats(src, st, mv, stat_sem, mv_sem, count):
                for j in range(TB):
                    last = dve.bn_stats(st[:, j, :], src[:, j, :])
                last.then_inc(s[stat_sem], 1)
                need(dve, s[stat_sem], count)
                dve.sem_inc(s["dve_waited"], 1)
                for j in range(TB):
                    last = dve.bn_aggr(mv[:, j, :], st[:, j, :])
                last.then_inc(s[mv_sem], 1)

            def neg_mean(mv, rs, nm, rs_sem, nm_sem, count):
                need(dve, s[rs_sem], count)
                dve.scalar_tensor_tensor(nm[:, :], mv[:, :, 0], -1.0, rs[:, :], ALU.mult,
                                         ALU.mult).then_inc(s[nm_sem], 1)

            def times_b(i, ip, n):
                need(dve, b_loaded[n // GN], 16 * (i + 1))
                need(dve, s["u_done"], i + 1)
                need(dve, s["scan_done"], KH * (NS * i + n - X_RING + 1))
                dve.tensor_tensor(dbx[:, n % X_RING, :, :], u[:, ip, :, :], b_of(n),
                                  ALU.mult).then_inc(s["dbx_vec"], 1)

            def scans(t, n):
                cols, sem_of = (VEC_COLS, "dbx_vec") if n in VEC_COLS else (POOL_COLS, "dbx_pool")
                need(dve, s[sem_of], len(cols) * t + made(cols, n))
                need(dve, s["carry_saved"], NS * (t - 1) + n + 1)
                need(dve, s["y_added"], NS * t + n - H_RING + 1)
                for h in range(KH):
                    need(dve, s["da_ready"], KH * (NS * t + n) + h + 1)
                    dve.tensor_tensor_scan(hg[:, n % H_RING, h, :], da_ps[:, (KH * n + h) % DA_BANKS, :],
                                           dbx[:, n % X_RING, h, :], carry[:, n, h:h + 1],
                                           ALU.mult, ALU.add).then_inc(s["scan_done"], 1)

            def keep_carry(t, par, n):
                need(dve, s["scan_done"], KH * (NS * t + n + 1))
                dve.tensor_scalar(carry[:, n, :], hg[:, n % H_RING, :, LC - 1], keep[:, par:par + 1], None,
                                  ALU.mult).then_inc(s["carry_saved"], 1)

            def step(t, par, pre=False, scan=False, mid=False, end=False):
                nxt = 1 - par

                def residual(v):
                    need(dve, s["post_ready"], post_count(t, f"wo{v}"))
                    need(dve, s["res_set"], t)
                    dve.tensor_tensor(res[:, 2 * v:2 * v + 2, :], post_tok, res[:, 2 * v:2 * v + 2, :],
                                      ALU.add).then_inc(s["post_read"], 1)

                def gate_v(v):
                    need(dve, s["sig_done"], t - 1)
                    need(dve, s["post_ready"], post_count(t, f"v{v}"))
                    dve.tensor_tensor(r_out[:, 2 * v:2 * v + 2, :], r_out[:, 2 * v:2 * v + 2, :], post_tok,
                                      ALU.mult).then_inc(s["post_read"], 1)

                for n in range(NS):
                    ahead = column_at(t, par, n + 1, scan, pre, mid)
                    if ahead and ahead[2] in VEC_COLS:
                        times_b(*ahead)
                    if scan:
                        scans(t, n)
                        if n == 0:
                            if not (isinstance(t, int) and t == 0):
                                keep_carry(t - 1, nxt, NS - 1)
                            if not (isinstance(t, int) and t == NT - 1):
                                dve.tensor_copy(keep[:, par:par + 1], notfirst[:, bass.ds(t + 1, 1)]).then_inc(s["keep_set"], 1)
                                need(dve, s["keep_set"], t + 1)
                                dve.sem_inc(s["dve_waited"], 1)
                        else:
                            keep_carry(t, par, n - 1)
                    if mid and isinstance(t, int) and t == NT and n == 0:
                        keep_carry(NT - 1, nxt, NS - 1)
                    if pre and n == 0:
                        need(dve, s["x_loaded"], 16 * (t + 2))
                        stats(x_tok, st1, mv1, "ln1_stat", "ln1_mv", t + 2)
                    if pre and n == 2:
                        neg_mean(mv1, rs1, nm1, "ln1_rs", "ln1_nm", t + 2)
                    if mid and n == 4:
                        need(dve, s["y_added"], NS * t)
                        for h in range(KH):
                            last = dve.scalar_tensor_tensor(gated[:, h, :], xT[:, nxt, h, :], d_par[:, h:h + 1],
                                                            y_ps[:, h, :], ALU.mult, ALU.add)
                        last.then_inc(s["y_read"], 1)
                        need(dve, s["y_read"], t)
                        need(dve, s["z_done"], t)
                        dve.tensor_tensor(gated[:, :, :], gated[:, :, :], zs[:, nxt, :, :],
                                          ALU.mult).then_inc(s["gated_done"], 1)
                    if mid and n == 6:
                        residual(0)
                    if mid and n == 7:
                        residual(1)
                        need(dve, s["post_read"], post_count(t, "wo1"))
                        stats(res, st2, mv2, "ln2_stat", "ln2_mv", t)
                        need(dve, s["ln2_mv"], t)
                        for j in range(TB):
                            last = dve.scalar_tensor_tensor(res[:, j, :], res[:, j, :], mv2[:, j, 0:1], g_all[:, :],
                                                            ALU.subtract, ALU.mult)
                        last.then_inc(s["ln2_g"], 1)
                    if end and n == 8:
                        gate_v(0)
                    if end and n == 9:
                        gate_v(1)
                        need(dve, s["post_read"], post_count(t, "v1"))
                        dve.tensor_tensor(r_out[:, :, :], r_out[:, :, :], xres[:, par, :, :],
                                          ALU.add).then_inc(s["ffn_done"], 1)
                    if mid and n == 9:
                        need(dve, s["xb_done"], t)
                        need(dve, s["ln2_rs"], t)
                        need(dve, s["ln2_g"], t)
                        for j in range(TB):
                            last = dve.scalar_tensor_tensor(xres[:, nxt, j, :], res[:, j, :], rs2[:, j:j + 1],
                                                            xres[:, nxt, j, :], ALU.mult, ALU.add)
                        last.then_inc(s["x2_done"], 1)
                        need(dve, s["x2_done"], t)
                        stats(xres[:, nxt, :, :], st3, mv3, "ln3_stat", "ln3_mv", t)
                    if mid and n == 11:
                        neg_mean(mv3, rs3, nm3, "ln3_rs", "ln3_nm", t)
                    if pre and n == 12:
                        need(dve, s["ln_done"], t + 2)
                        dve.scalar_tensor_tensor(one_e[:, :, :].rearrange("p k l -> p (k l)"),
                                                 one_e[:, :, :].rearrange("p k l -> p (k l)"), 1.0,
                                                 abs_v[:, :, :].rearrange("p k l -> p (k l)"),
                                                 ALU.subtract, ALU.subtract).then_inc(s["nc_done"], 1)
                        need(dve, s["nc_done"], t + 2)
                        dve.scalar_tensor_tensor(relu_v[:, :, :].rearrange("p k l -> p (k l)"),
                                                 relu_v[:, :, :].rearrange("p k l -> p (k l)"), ln_of_1[:, 0:1],
                                                 one_e[:, :, :].rearrange("p k l -> p (k l)"),
                                                 ALU.subtract, ALU.subtract).then_inc(s["rl_done"], 1)
                        need(dve, s["rl_done"], t + 2)
                        dve.tensor_tensor(delta[:, nxt, :, :], relu_v[:, :, :], ln_v[:, :, :],
                                          ALU.add).then_inc(s["delta_done"], 1)
                    if mid and n == 12:
                        need(dve, s["mixed"], t - 1)
                        dve.tensor_scalar(hT[:, :, 0], hT[:, :, LC], notfirst[:, bass.ds(t - 1, 1)], None,
                                          ALU.mult).then_inc(s["prev_done"], 1)
                    if pre and n == 13:
                        need(dve, s["delta_done"], t + 2)
                        dve.tensor_tensor(u[:, nxt, :, :], delta[:, nxt, :, :], xT[:, nxt, :, :],
                                          ALU.mult).then_inc(s["u_done"], 1)
                    if mid and n == 15:
                        need(dve, s["mixed_prev"], t)
                        for mix, mu in ((xk, muk), (xr, mur)):
                            for k in range(KH):
                                last = dve.scalar_tensor_tensor(mix[:, k, :], hT[:, k, 1:LC + 1], mu[:, k:k + 1],
                                                                mix[:, k, :], ALU.mult, ALU.add)
                        last.then_inc(s["mixed"], 1)

            steps(dve, step)

        @block.tensor
        def _(pe):
            pe.wait_ge(s["ident_done"], 1)
            pe.wait_ge(s["w_loaded"], 16 * 15)
            for n, src in enumerate([wx_raw] + raw):
                bank = (pre_ps, post_ps)[n % 2]
                if n >= 2:
                    pe.wait_ge(s["setup_ev"], n - 1)
                for k in range(KH):
                    for m in range(KH):
                        last = pe.transpose(bank[:, m * D + k * P:m * D + k * P + P], src[:, k, m * P:(m + 1) * P],
                                            ident[:, :])
                last.then_inc(s["setup_pe"], 1)
            pe.wait_ge(s["setup_ev"], 3)
            for m in range(KH):
                for k in range(KH):
                    last = pe.matmul(pre_ps[:, m * D:(m + 1) * D], wxT[:, k, m * P:(m + 1) * P], wdt_raw[:, k, :],
                                     start=k == 0, stop=k == KH - 1)
            last.then_inc(s["setup_pe"], 1)
            pe.wait_ge(s["setup_ev"], 5)

            def add_up(i, n):
                need(pe, s["g_ready"], NS * i + n + 1)
                if n == 0:
                    need(pe, s["y_read"], i)
                for h in range(KH):
                    last = pe.matmul(y_ps[:, h, :], ident[:, :], hg[:, n % H_RING, h, :],
                                     start=n == 0, stop=n == NS - 1)
                last.then_inc(s["y_added"], 1)

            def project(out, w, x, cols):
                for k in range(KH):
                    last = pe.matmul(out, w[:, k, cols], x[:, k, :], start=k == 0, stop=k == KH - 1)
                return last

            def by_token(v, xT_, w):
                for b in range(2):
                    for k in range(KH):
                        last = pe.matmul(post_tok[:, b, :], xT_[:, k, (2 * v + b) * P:(2 * v + b + 1) * P], w[:, k, :],
                                         start=k == 0, stop=k == KH - 1)
                return last

            def turned(bank, src, k):
                for j in range(TB):
                    last = pe.transpose(bank[:, j * P:(j + 1) * P], src[:, j, k * P:(k + 1) * P], ident[:, :])
                return last

            def step(t, par, pre=False, scan=False, mid=False, end=False):
                nxt = 1 - par
                i = t + 1

                def pre_unit(unit):
                    need(pe, s["pre_read"], pre_count(i, unit) - 1)
                    m = int(unit[-1]) if unit != "bc" else 0
                    cols = slice(m * P, (m + 1) * P)
                    if unit in ("xnT0", "xnT1"):
                        need(pe, s["xn_done"], i + 1)
                        last = turned(pre_ps, xn_tok[:, nxt, :, :], m)
                    elif unit in ("x0", "x1"):
                        last = project(pre_ps[:, :], w_in, xnT, cols)
                    elif unit in ("z0", "z1"):
                        last = project(pre_ps[:, :], w_in, xnT, slice(D + m * P, D + (m + 1) * P))
                    elif unit == "bc":
                        last = project(pre_ps[0:2 * NS, :], w_bc, xT[:, nxt, :, :], slice(0, 2 * NS))
                    else:
                        last = project(pre_ps[:, :], w_dtx, xT[:, nxt, :, :], cols)
                    last.then_inc(s["pre_ready"], 1)

                def post_unit(unit):
                    need(pe, s["post_read"], post_count(t, unit) - 1)
                    m = int(unit[-1])
                    cols = slice(m * P, (m + 1) * P)
                    if unit[:2] == "wo":
                        need(pe, s["gated_done"], t)
                        last = by_token(m, gated, w_out)
                    elif unit[:2] == "hT":
                        need(pe, s["hn_done"], t)
                        last = turned(post_ps, res, m)
                    elif unit[0] == "k":
                        need(pe, s["mixed"], t - 1)
                        last = project(post_ps[:, :], w_kT, xk, cols)
                    elif unit[0] == "r":
                        last = by_token(m, xr, w_rT)
                    else:
                        need(pe, s["kact_done"], t - 1)
                        last = by_token(m, kact, w_vT)
                    last.then_inc(s["post_ready"], 1)

                at = {0: ["k0"], 1: ["k1"], 2: ["r0"], 3: ["r1", "xnT0"], 4: ["xnT1"], 5: ["wo0"], 6: ["x0", "wo1"],
                      7: ["x1", "v0"], 8: ["bc", "v1"], 9: ["dt0"], 10: ["dt1"], 11: ["z0"], 12: ["z1", "hT0"],
                      13: ["hT1"]}
                for n in range(NS):
                    for unit in at.get(n, ()):
                        if unit in PRE and pre:
                            pre_unit(unit)
                        if (unit in POST_A and mid) or (unit in POST_B and end):
                            post_unit(unit)
                    behind = column_at(t, par, n - Y_LAG, scan, pre, mid)
                    if behind:
                        add_up(behind[0], behind[2])

            steps(pe, step)


_INS = ["L0_attn_x_in", "L0_attn_W_in", "L0_attn_W_x", "L0_attn_W_dt", "L0_attn_b_dt", "L0_attn_A_log",
        "L0_attn_D_param", "L0_attn_W_out", "L0_attn_ln_g", "L0_attn_ln_b", "L0_ffn_W_r", "L0_ffn_W_k",
        "L0_ffn_W_v", "L0_ffn_mu_r", "L0_ffn_mu_k"]
_OUT = ((BATCH, LEN, D), "float32")


def kernel(**inputs):
    import numpy as _np
    import concourse.bacc as _bacc
    from concourse import mybir as _mybir
    from concourse.bass_utils import run_bass_kernel_spmd as _run

    nc = _bacc.Bacc("TRN2", target_bir_lowering=False, num_devices=1)
    arrays, args = {}, []
    for name in _INS:
        a = _np.ascontiguousarray(inputs[name])
        arrays[f"in_{name}_dram"] = a
        args.append(nc.dram_tensor(f"in_{name}_dram", a.shape, _mybir.dt.from_np(a.dtype), kind="ExternalInput").ap())
    shape, dtype = _OUT
    args.append(nc.dram_tensor("out_0_dram", shape, _mybir.dt.from_np(_np.dtype(dtype)), kind="ExternalOutput").ap())
    mamba_rwkv_layer(nc, *args)
    r = _run(nc, [arrays], core_ids=[0])
    return r.results[0]["out_0_dram"]
```

```python
from contextlib import ExitStack

import concourse.bass as bass
from concourse import mybir

P = 128
BATCH, LEN, D = 4, 2048, 256
NS = 16
LC = 512
TB = LC // P
KH = D // P
CPB = LEN // LC
NT = BATCH * CPB
EPS = 1e-5
GN = 4
GROUPS = NS // GN
BG = 2
X_RING = 4
H_RING = 8
DA_BANKS = 4
B_LEAD, C_LAG, Y_LAG = 2, 2, 4
LAST_VEC_C = [3, 5, 9, 12, 14, 15]

F32 = mybir.dt.float32
ALU = mybir.AluOpType
ACT = mybir.ActivationFunctionType

POOL_COLS = [1, 2, 6, 8, 11, 12, 13, 14]
VEC_COLS = [n for n in range(NS) if n not in POOL_COLS]


POOL_TURN = dict(xb=4, rs2=6, rs13=11)
ACT_TURN = dict(norm1=2, xnT0=3, xnT1=4, x0=6, x1=8, bc=8, dt0=9, dt1=11, softplus=11, z0=11, z1=14, k0=1, k1=2,
                square=5, r0=4, r1=6, sigmoid=6, silu=6, res_copy=1, norm2=8, norm3=12, hT0=14, hT1=15,
                mix_prev=15)
VEC_TURN = dict(mix_k=0, mix_r=0, nm1=0, gate=4, res0=6, res1=7, stats2=7, nm2=8, gv0=10, gv1=11, out=11,
                log1p=11, relu=12, delta=13, u=13, gain=9, x2=10, stats3=10, nm3=12, hT_prev=3, stats1=5, rs13=12)
PE_TURN = dict(k0=1, k1=2, r0=3, r1=4, xnT0=3, xnT1=4, wo0=5, wo1=6, x0=5, x1=7, bc=8, dt0=8, dt1=9, z0=11, z1=12,
               v0=8, v1=10, hT0=14, hT1=15, xD=11)

VEC_LAST = dict(VEC_TURN, mix_k=1, mix_r=1, gate=4, res0=4, res1=6, stats2=6, nm2=6, gain=7, x2=10, stats3=10,
                hT_prev=8, nm3=11, gv0=15, gv1=15, out=15)
PE_LAST = dict(PE_TURN, wo0=4, wo1=6, k0=8, k1=11, r0=7, r1=9, v0=12, v1=12, hT0=13, hT1=14)
ACT_LAST = dict(ACT_TURN, res_copy=4, k0=6, k1=8, square=10, r0=5, r1=8, sigmoid=10, norm2=7, norm3=12, hT0=13,
                hT1=15, mix_prev=15)


def made(cols, n):
    return sum(c <= n for c in cols)


def need(eng, sem, count):
    if not (isinstance(count, int) and count <= 0):
        eng.wait_ge(sem, count)


def mamba_rwkv_layer(nc, x_in, W_in, W_x, W_dt, b_dt, A_log, D_param, W_out, ln_g, ln_b,
                     W_r, W_k, W_v, mu_r, mu_k, out):
    x_v = x_in.rearrange("b (c j p) d -> (b c) p j d", p=P, j=TB)
    out_v = out.rearrange("b (c j p) d -> (b c) p j d", p=P, j=TB)
    bc_dram = nc.dram_tensor("bc_rows_dram", (NT, 2 * NS, LC), F32).ap()

    def halves(w):
        return w.rearrange("(k p) n -> p k n", p=P)

    def column(v):
        return v.rearrange("(k p) -> p k", p=P)

    with ExitStack() as ctx:
        def sb(name, *shape):
            return ctx.enter_context(nc.sbuf_tensor(name, list(shape), F32))

        def ps(name, *shape):
            return ctx.enter_context(nc.psum_tensor(name, list(shape), F32))

        def sem(name):
            return ctx.enter_context(nc.semaphore(name))

        ident = sb("ident", P, P)
        w_in = sb("w_in", P, KH, 2 * D)
        w_bc = sb("w_bc", P, KH, 2 * NS)
        w_dtx = sb("w_dtx", P, KH, D)
        w_out = sb("w_out", P, KH, D)
        w_rT = sb("w_rT", P, KH, D)
        w_kT = sb("w_kT", P, KH, D)
        w_vT = sb("w_vT", P, KH, D)
        bdt = sb("bdt", P, KH)
        a_neg = sb("a_neg", P, KH, NS)
        d_par = sb("d_par", P, KH)
        diag_d = sb("diag_d", P, KH, P)
        mur = sb("mur", P, KH)
        muk = sb("muk", P, KH)
        omr = sb("omr", P, KH)
        omk = sb("omk", P, KH)
        g_all = sb("g_all", P, D)
        b_all = sb("b_all", P, D)
        notfirst = sb("notfirst", P, NT)
        ln_of_1 = sb("ln_of_1", P, 1)
        neg_half = sb("neg_half", P, TB)
        x_tok = sb("x_tok", P, TB, D)
        xn_tok = sb("xn_tok", P, 2, TB, D)
        xnT = sb("xnT", P, KH, LC)
        xT = sb("xT", P, 2, KH, LC)
        zs = sb("zs", P, 2, KH, LC)
        bc_rows = sb("bc_rows", 2 * NS, LC)
        relu_v = sb("relu_v", P, KH, LC)
        ln_v = sb("ln_v", P, KH, LC)
        one_e = sb("one_e", P, KH, LC)
        abs_v = sb("abs_v", P, KH, LC)
        delta = sb("delta", P, 2, KH, LC)
        u = sb("u", P, 2, KH, LC)
        st1 = sb("st1", P, TB, 6)
        mv1 = sb("mv1", P, TB, 2)
        ve13 = sb("ve13", P, 2, TB)
        rs13 = sb("rs13", P, 2, TB)
        rs_first = sb("rs_first", P, 2, TB)
        rs_step = sb("rs_step", P, 2, TB)
        nm1 = sb("nm1", P, TB)
        b_ring = sb("b_ring", P, BG, GN, LC)
        c_ring = sb("c_ring", P, BG, GN, LC)
        dbx = sb("dbx", P, X_RING, KH, LC)
        hg = sb("hg", P, H_RING, KH, LC)
        carry = sb("carry", P, NS, KH)
        keep = sb("keep", P, 2)
        xres = sb("xres", P, 2, TB, D)
        gated = sb("gated", P, KH, LC)
        res = sb("res", P, TB, D)
        st2 = sb("st2", P, TB, 6)
        mv2 = sb("mv2", P, TB, 2)
        rs2 = sb("rs2", P, TB)
        nm2 = sb("nm2", P, TB)
        st3 = sb("st3", P, TB, 6)
        mv3 = sb("mv3", P, TB, 2)
        nm3 = sb("nm3", P, TB)
        hT = sb("hT", P, KH, LC + 1)
        xr = sb("xr", P, KH, LC)
        xk = sb("xk", P, KH, LC)
        kact = sb("kact", P, KH, LC)
        r_out = sb("r_out", P, TB, D)
        W_LOADS = 12
        wx_raw = c_ring[:, 0, 0:1, :].rearrange("p a (k n) -> p (a k) n", k=KH)
        wdt_raw = c_ring[:, 0, 1:2, :].rearrange("p a (k n) -> p (a k) n", k=KH)
        wxT = c_ring[:, 0, 2:3, :].rearrange("p a (k n) -> p (a k) n", k=KH)
        raw = [hg[:, H_RING - 1 - m, 0:1, :].rearrange("p a (k n) -> p (a k) n", k=KH) for m in range(3)]

        y_ps = ps("y_ps", P, KH, LC)
        da_ps = ps("da_ps", P, DA_BANKS, LC)
        pre_ps = ps("pre_ps", P, LC)
        post_ps = ps("post_ps", P, LC)
        START_BANKS = [da_ps[:, m, :] for m in range(DA_BANKS)] + [y_ps[:, m, :] for m in range(KH)]

        names = """w_in_loaded w_dt_loaded w_loaded ident0 ident_done flags0 flags_done half_done
            a_exped a_set omu_set diag_set dve_waited sp_waited setup_pe setup_ev ln1_done
            x_loaded xres_loaded bc_stored out_stored
            ln1_stat ln1_mv ln1_ve rs_ln rs_first_done rs_sq rs_sqv ln13_rs ln1_nm xn_done pre_ready pre_read bc_rows_done
            abs_done exp_done ln_done nc_done rl_done delta_done u_done
            keep_set scan_done carry_saved da_ready dbx_vec dbx_pool g_ready g_last_ready y_added
            gated_done z_done post_ready post_read tail_read0 tail_read1 res_set xb_done
            ln2_stat ln2_mv ln2_ve ln2_rs ln2_nm res_normed ln2_g x2_done
            ln3_stat ln3_mv ln3_ve ln3_nm hn_done prev_done mixed_prev_k mixed_prev_r mixed_k mixed_r
            kact_done sig_done ffn_done""".split()
        s = {name: sem(name) for name in names}
        b_loaded = [sem(f"b_loaded{g}") for g in range(GROUPS)]
        c_loaded = [sem(f"c_loaded{g}") for g in range(GROUPS)]
        block = ctx.enter_context(nc.Block())

        def turns(table, last, t):
            return last if isinstance(t, int) and t == NT else table

        PRE = sorted(["xnT0", "xnT1", "x0", "x1", "bc", "dt0", "dt1", "z0", "z1"], key=PE_TURN.get)
        POST = sorted(["k0", "k1", "r0", "r1", "wo0", "wo1", "v0", "v1", "hT0", "hT1"], key=PE_TURN.get)
        POST_LAST = sorted(POST, key=PE_LAST.get)
        POST_A = [unit for unit in POST if unit[:2] in ("wo", "hT")]
        POST_B = [unit for unit in POST if unit not in POST_A]

        def pre_count(i, unit):
            return len(PRE) * i + PRE.index(unit) + 1

        def post_count(t, unit):
            if isinstance(t, int) and t == 1:
                return POST_A.index(unit) + 1
            if isinstance(t, int) and t == NT + 1:
                return len(POST_A) + len(POST) * (NT - 1) + POST_B.index(unit) + 1
            order = POST_LAST if isinstance(t, int) and t == NT else POST
            return len(POST) * (t - 2) + len(POST_A) + order.index(unit) + 1

        def ln13(part, mid, more):
            return part[:, 0 if more else 1:2 if mid else 1, :]

        def bank(t, unit):
            if isinstance(t, int) and t == -1:
                return START_BANKS[PRE.index(unit) % len(START_BANKS)]
            return pre_ps

        def post_bank(t, unit):
            at = tail_index(t, unit)
            return post_ps if at is None else (pre_ps, post_ps)[at % 2]

        def tail_index(t, unit):
            if isinstance(t, int) and t >= NT:
                return post_count(t, unit) - post_count(NT, POST_LAST[0])

        def read_sem(t, unit):
            at = tail_index(t, unit)
            return s["post_read"] if at is None else s[f"tail_read{at % 2}"]

        def need_read(eng, t, unit, before=0):
            at = tail_index(t, unit)
            if at is None:
                need(eng, s["post_read"], post_count(t, unit) - before)
            elif at < before:
                need(eng, s["post_read"], post_count(t, unit) - before)
            else:
                need(eng, s[f"tail_read{(at - before) % 2}"], (at - before) // 2 + 1)

        def by_block(b):
            return b[:, :].rearrange("p (s d) -> p s d", d=D)

        def vec_c(i, n):
            return isinstance(i, int) and i == NT - 1 and n in LAST_VEC_C

        def steps(eng, step):
            step(-1, 1, pre=True, more=True)
            step(0, 0, pre=True, scan=True, more=True)
            step(1, 1, pre=True, scan=True, mid=True, more=True)
            with eng.Fori(0, (NT - 4) // 2) as pair:
                step(2 * pair + 2, 0, pre=True, scan=True, mid=True, end=True, more=True)
                step(2 * pair + 3, 1, pre=True, scan=True, mid=True, end=True, more=True)
            step(NT - 2, 0, pre=True, scan=True, mid=True, end=True)
            step(NT - 1, 1, scan=True, mid=True, end=True)
            step(NT, 0, mid=True, end=True)
            step(NT + 1, 1, end=True)

        def column_at(t, par, n, scan, pre, mid):
            if n >= NS:
                return (t + 1, 1 - par, n - NS) if pre else None
            if n < 0:
                return (t - 1, 1 - par, n + NS) if mid else None
            return (t, par, n) if scan else None

        def b_of(n):
            return b_ring[:, n // GN % BG, n % GN:n % GN + 1, :].to_broadcast([P, KH, LC])

        def flat(a):
            return a[:, :, :].rearrange("p k l -> p (k l)")

        def c_of(n):
            return c_ring[:, n // GN % BG, n % GN:n % GN + 1, :].to_broadcast([P, KH, LC])

        @block.sync
        def _(sp):
            sp.dma_start(x_tok[:, :, :], x_v[0]).then_inc(s["x_loaded"], 16)
            sp.dma_start(w_in[:, :, :], halves(W_in)).then_inc(s["w_in_loaded"], 16)
            sp.dma_start(wx_raw, halves(W_x)[:, :, 0:D]).then_inc(s["w_dt_loaded"], 16)
            sp.dma_start(wdt_raw, halves(W_dt)).then_inc(s["w_dt_loaded"], 16)
            loads = [(w_bc[:, :, :], halves(W_x)[:, :, D:]), (a_neg[:, :, :], halves(A_log)),
                     (raw[0], halves(W_r)), (raw[1], halves(W_k)), (raw[2], halves(W_v)),
                     (w_out[:, :, :], halves(W_out))]
            loads += [(dst[:, :], v.rearrange("(o d) -> o d", o=1).partition_broadcast(P))
                      for dst, v in ((g_all, ln_g), (b_all, ln_b))]
            for dst, v in ((bdt, b_dt), (d_par, D_param), (mur, mu_r), (muk, mu_k)):
                sp.dma_start(dst[:, :], column(v), allow_slow_non_contiguous=True).then_inc(s["w_loaded"], 16)
            for dst, src in loads:
                sp.dma_start(dst, src).then_inc(s["w_loaded"], 16)

            def arrived(sem, count):
                need(sp, sem, count)
                sp.sem_inc(s["sp_waited"], 1)

            def slot_before(i, g):
                return (i, g - BG) if g >= BG else (i - 1, g + BG)

            def load_b(i, g, first=False):
                if not first:
                    before, at = slot_before(i, g)
                    last = GN * at + GN - 1
                    arrived(s["dbx_vec"], len(VEC_COLS) * before + made(VEC_COLS, last))
                    arrived(s["dbx_pool"], len(POOL_COLS) * before + made(POOL_COLS, last))
                sp.dma_start(b_ring[:, g % BG, :, :],
                             bc_dram[i, GN * g:GN * g + GN, :].partition_broadcast(P)).then_inc(b_loaded[g], 16)

            def load_c(i, g, first=False):
                if not first:
                    before, at = slot_before(i, g)
                    columns = GN * at + GN
                    if isinstance(i, int) and before == NT - 1:
                        on_vec = made(LAST_VEC_C, columns - 1)
                        columns -= on_vec
                        arrived(s["g_last_ready"], on_vec)
                    arrived(s["g_ready"], NS * before + columns)
                sp.dma_start(c_ring[:, g % BG, :, :],
                             bc_dram[i, NS + GN * g:NS + GN * g + GN, :].partition_broadcast(P)).then_inc(c_loaded[g], 16)

            def step(t, par, pre=False, scan=False, mid=False, end=False, more=False):
                start = isinstance(t, int) and t == -1
                if mid:
                    arrived(s["ffn_done"], t - 2)
                    arrived(s["x2_done"], t - 1)
                    sp.dma_start(xres[:, 1 - par, :, :], x_v[t - 1]).then_inc(s["xres_loaded"], 16)
                if scan:
                    if not (isinstance(t, int) and t == 0):
                        load_c(t, 1)
                if more:
                    arrived(s["xn_done"], t + 2)
                    sp.dma_start(x_tok[:, :, :], x_v[t + 2]).then_inc(s["x_loaded"], 16)
                if scan:
                    load_b(t, 2)
                    load_c(t, 2)
                    load_b(t, 3)
                if pre:
                    arrived(s["bc_rows_done"], t + 2)
                    sp.dma_start(bc_dram[t + 1], bc_rows[:, :]).then_inc(s["bc_stored"], 16)
                if end:
                    ended = isinstance(t, int) and t == NT + 1
                    for m, blocks in enumerate([slice(0, TB // 2), slice(TB // 2, TB)] if ended else [slice(0, TB)]):
                        arrived(s["ffn_done"], t - 1 + m)
                        sp.dma_start(out_v[t - 2][:, blocks, :], r_out[:, blocks, :]).then_inc(s["out_stored"], 16)
                if scan:
                    load_c(t, 3)
                if pre:
                    arrived(s["bc_stored"], 16 * (t + 2))
                    if start:
                        arrived(s["setup_ev"], 2)
                    load_b(t + 1, 0, start)
                    load_c(t + 1, 0, start)
                    load_b(t + 1, 1, start)
                    if start:
                        load_c(0, 1, True)

            steps(sp, step)
            sp.wait_ge(s["out_stored"], 16 * (NT + 1))

        @block.gpsimd
        def _(pool):
            pool.memset(ident[:, :], 0.0).then_inc(s["ident0"], 1)
            pool.wait_ge(s["ident0"], 1)
            pool.affine_select(out=ident[:, :], in_=ident[:, :], compare_op=ALU.not_equal, fill=1.0, base=0,
                               pattern=[[-1, P]], channel_multiplier=1).then_inc(s["ident_done"], 1)

            pool.memset(neg_half[:, :], -0.5).then_inc(s["half_done"], 1)
            pool.wait_ge(s["half_done"], 1)

            def rsqrt(rs, ve):
                return pool.tensor_tensor(rs, ve, neg_half[:, :], ALU.pow)

            def times_b(i, ip, n):
                need(pool, b_loaded[n // GN], 16 * (i + 1))
                need(pool, s["u_done"], i + 1)
                need(pool, s["scan_done"], KH * (NS * i + n - X_RING + 1))
                pool.tensor_tensor(dbx[:, n % X_RING, :, :], u[:, ip, :, :], b_of(n),
                                   ALU.mult).then_inc(s["dbx_pool"], 1)

            def times_c(i, n):
                need(pool, c_loaded[n // GN], 16 * (i + 1))
                if isinstance(i, int) and i == 0 and n == 0:
                    pool.wait_ge(s["w_loaded"], 16 * W_LOADS)
                need(pool, s["carry_saved"], NS * i + n + 1)
                pool.tensor_tensor(hg[:, n % H_RING, :, :], hg[:, n % H_RING, :, :], c_of(n),
                                   ALU.mult).then_inc(s["g_ready"], 1)

            def step(t, par, pre=False, scan=False, mid=False, end=False, more=False):
                nxt = 1 - par
                if isinstance(t, int) and t == -1:
                    pool.wait_ge(s["ln1_ve"], 1)
                    rsqrt(rs13[:, 0, :], ve13[:, 0, :]).then_inc(s["ln13_rs"], 1)
                for n in range(NS):
                    ahead = column_at(t, par, n + B_LEAD, scan, pre, mid)
                    if ahead and ahead[2] in POOL_COLS:
                        times_b(*ahead)
                    behind = column_at(t, par, n - C_LAG, scan, pre, mid)
                    if behind and not vec_c(behind[0], behind[2]):
                        times_c(behind[0], behind[2])
                    if mid and n == POOL_TURN["xb"]:
                        need(pool, s["xres_loaded"], 16 * t)
                        pool.tensor_tensor(xres[:, nxt, :, :], xres[:, nxt, :, :],
                                           b_all[:, :].unsqueeze(1).to_broadcast([P, TB, D]),
                                           ALU.add).then_inc(s["xb_done"], 1)
                    if mid and n == POOL_TURN["rs2"]:
                        need(pool, s["ln2_ve"], t)
                        rsqrt(rs2[:, :], rs2[:, :]).then_inc(s["ln2_rs"], 1)
                    if mid and not pre and n == POOL_TURN["rs13"]:
                        need(pool, s["ln3_ve"], t)
                        rsqrt(rs13[:, 1, :], ve13[:, 1, :]).then_inc(s["ln13_rs"], 1)

            steps(pool, step)

        @block.scalar
        def _(act):
            act.wait_ge(s["flags_done"], 3)
            act.activation(ln_of_1[:, :], notfirst[:, 0:1], ACT.Ln, scale=0.0, bias=1.0).then_inc(s["ln1_done"], 1)

            def norm(dst, src, rs, nm, done):
                for j in range(TB):
                    last = act.activation(dst[:, j, :], src[:, j, :], ACT.Identity,
                                          scale=rs[:, j:j + 1], bias=nm[:, j:j + 1])
                last.then_inc(s[done], 1)

            def exps(i, ip, n):
                need(act, s["delta_done"], i + 1)
                if isinstance(i, int) and i == 0 and n == 0:
                    act.wait_ge(s["pre_read"], len(PRE))
                for h in range(KH):
                    need(act, s["scan_done"], KH * (NS * i + n) + h - DA_BANKS + 1)
                    act.activation(da_ps[:, (KH * n + h) % DA_BANKS, :], delta[:, ip, h, :], ACT.Exp,
                                   scale=a_neg[:, h, n:n + 1]).then_inc(s["da_ready"], 1)

            def keep_carries(t, par, n):
                need(act, s["scan_done"], KH * (NS * t + n + 1))
                if not (isinstance(t, int) and t == NT - 1):
                    need(act, s["keep_set"], t + 1)
                slot = (n - 1) % H_RING
                act.activation(carry[:, n - 1:n + 1, :], hg[:, slot:slot + 2, :, LC - 1], ACT.Copy,
                               scale=keep[:, par:par + 1]).then_inc(s["carry_saved"], 2)

            def step(t, par, pre=False, scan=False, mid=False, end=False, more=False):
                nxt = 1 - par

                def from_pre(unit, dst):
                    need(act, s["pre_ready"], pre_count(t + 1, unit))
                    act.activation(dst, bank(t, unit)[:, :], ACT.Copy).then_inc(s["pre_read"], 1)

                def relu_k(m):
                    need(act, s["post_ready"], post_count(t, f"k{m}"))
                    act.activation(kact[:, m, :], post_bank(t, f"k{m}")[:, :],
                                   ACT.Relu).then_inc(read_sem(t, f"k{m}"), 1)

                def raw_r(v):
                    need(act, s["out_stored"], 16 * (t - 2))
                    need(act, s["post_ready"], post_count(t, f"r{v}"))
                    act.activation(r_out[:, 2 * v:2 * v + 2, :], by_block(post_bank(t, f"r{v}")),
                                   ACT.Copy).then_inc(read_sem(t, f"r{v}"), 1)

                def softplus_in(m):
                    need(act, s["pre_ready"], pre_count(t + 1, f"dt{m}"))
                    v = bank(t, f"dt{m}")
                    act.activation(abs_v[:, m, :], v[:, :], ACT.Abs, bias=bdt[:, m:m + 1]).then_inc(s["abs_done"], 1)
                    act.activation(relu_v[:, m, :], v[:, :], ACT.Relu, bias=bdt[:, m:m + 1]).then_inc(s["pre_read"], 1)

                def at(stage):
                    return n == turns(ACT_TURN, ACT_LAST, t)[stage]

                for n in range(NS):
                    ahead = column_at(t, par, n + 1, scan, pre, mid)
                    if ahead:
                        exps(*ahead)
                    if n == 0 and mid:
                        keep_carries(t - 1, nxt, NS - 1)
                    if scan and n > 0 and n % 2 == 0:
                        keep_carries(t, par, n - 1)
                    if mid and at("res_copy"):
                        need(act, s["post_ready"], post_count(t - 1, "hT1") if not isinstance(t, int) or t > 1 else 0)
                        act.activation(res[:, :, :], xn_tok[:, nxt, :, :], ACT.Copy).then_inc(s["res_set"], 1)
                    if pre and at("norm1"):
                        need(act, s["ln1_nm"], t + 2)
                        need(act, s["res_set"], t)
                        norm(xn_tok[:, nxt, :, :], x_tok, rs13[:, 0, :], nm1, "xn_done")
                        if isinstance(t, int) and t == -1:
                            act.wait_ge(s["w_loaded"], 16 * W_LOADS)
                            act.activation(one_e[:, 0, 0:KH * NS], a_neg[:, :, :].rearrange("p k n -> p (k n)"),
                                           ACT.Exp).then_inc(s["a_exped"], 1)
                    for m in range(2):
                        if end and at(f"k{m}"):
                            relu_k(m)
                    if end and at("square"):
                        need_read(act, t, "k0")
                        need_read(act, t, "k1")
                        act.activation(kact[:, :, :], kact[:, :, :], ACT.Square).then_inc(s["kact_done"], 1)
                    for m in range(2):
                        if pre and at(f"xnT{m}"):
                            from_pre(f"xnT{m}", xnT[:, m, :])
                        if end and at(f"r{m}"):
                            raw_r(m)
                    if end and at("sigmoid"):
                        need_read(act, t, "r0")
                        need_read(act, t, "r1")
                        act.activation(r_out[:, :, :], r_out[:, :, :], ACT.Sigmoid).then_inc(s["sig_done"], 1)
                    if scan and at("silu"):
                        need(act, s["pre_read"], pre_count(t, PRE[-1]))
                        act.activation(zs[:, par, :, :], zs[:, par, :, :], ACT.Silu).then_inc(s["z_done"], 1)
                    for m in range(2):
                        if pre and at(f"x{m}"):
                            need(act, s["gated_done"], t)
                            from_pre(f"x{m}", xT[:, nxt, m, :])
                    if pre and at("bc"):
                        need(act, s["pre_ready"], pre_count(t + 1, "bc"))
                        need(act, s["bc_stored"], 16 * (t + 1))
                        act.activation(bc_rows[:, :], bank(t, "bc")[0:2 * NS, :], ACT.Copy).then_inc(s["pre_read"], 1)
                        need(act, s["pre_read"], pre_count(t + 1, "bc"))
                        act.sem_inc(s["bc_rows_done"], 1)
                    for m in range(2):
                        if pre and at(f"dt{m}"):
                            softplus_in(m)
                    if pre and at("softplus"):
                        need(act, s["abs_done"], KH * (t + 2))
                        act.activation(abs_v[:, :, :], abs_v[:, :, :], ACT.Exp, scale=-1.0).then_inc(s["exp_done"], 1)
                        need(act, s["exp_done"], t + 2)
                        if isinstance(t, int) and t == -1:
                            act.wait_ge(s["a_set"], 1)
                        act.activation(one_e[:, :, :], abs_v[:, :, :], ACT.Copy, bias=1.0)
                        act.activation(ln_v[:, :, :], abs_v[:, :, :], ACT.Ln, bias=1.0).then_inc(s["ln_done"], 1)
                        if more:
                            need(act, s["ln1_ve"], t + 3)
                        if mid:
                            need(act, s["ln3_ve"], t)
                        need(act, s["ln13_rs"], t + 2)
                        first = ln13(rs_first, mid, more)
                        act.activation(first, ln13(ve13, mid, more), ACT.Ln).then_inc(s["rs_ln"], 1)
                        need(act, s["rs_ln"], t + 2)
                        act.activation(first, first, ACT.Exp, scale=-0.5).then_inc(s["rs_first_done"], 1)
                    if mid and at("norm2"):
                        need(act, s["ln2_nm"], t)
                        norm(res, res, rs2, nm2, "res_normed")
                    for m in range(2):
                        if pre and at(f"z{m}"):
                            from_pre(f"z{m}", zs[:, nxt, m, :])
                    if isinstance(t, int) and t == -1 and at("z1"):
                        for m, w in enumerate((w_rT, w_kT, w_vT)):
                            act.wait_ge(s["setup_pe"], 3 + m)
                            turned = (pre_ps, post_ps)[m % 2][:, :].rearrange("p (k n) -> p k n", k=KH)
                            act.activation(w[:, :, :], turned, ACT.Copy).then_inc(s["setup_ev"], 1)
                    if mid and at("norm3"):
                        need(act, s["ln3_nm"], t)
                        need(act, s["ln2_g"], t)
                        norm(res, xres[:, nxt, :, :], rs13[:, 1, :], nm3, "hn_done")
                    for m in range(2):
                        if mid and at(f"hT{m}"):
                            need(act, s["prev_done"], t)
                            need(act, s["post_ready"], post_count(t, f"hT{m}"))
                            act.activation(hT[:, m, 1:LC + 1], post_bank(t, f"hT{m}")[:, :],
                                           ACT.Copy).then_inc(read_sem(t, f"hT{m}"), 1)
                    if mid and at("mix_prev"):
                        need_read(act, t, "hT0")
                        need_read(act, t, "hT1")
                        for mix, share, done in ((xk, omk, "mixed_prev_k"), (xr, omr, "mixed_prev_r")):
                            for k in range(KH):
                                last = act.activation(mix[:, k, :], hT[:, k, 0:LC], ACT.Copy, scale=share[:, k:k + 1])
                            last.then_inc(s[done], 1)

            steps(act, step)

        @block.vector
        def _(dve):
            dve.memset(notfirst[:, :], 1.0).then_inc(s["flags0"], 1)
            dve.wait_ge(s["flags0"], 1)
            dve.memset(notfirst[:, 0:NT:CPB], 0.0).then_inc(s["flags_done"], 1)
            dve.memset(carry[:, :, :], 0.0).then_inc(s["flags_done"], 1)
            dve.memset(hT[:, :, LC:LC + 1], 0.0).then_inc(s["flags_done"], 1)

            def turned_weight(m, dst):
                dve.wait_ge(s["setup_pe"], m + 1)
                dve.tensor_copy(dst, (pre_ps, post_ps)[m % 2][:, :].rearrange("p (k n) -> p k n",
                                                                              k=KH)).then_inc(s["setup_ev"], 1)

            def small_constants():
                dve.wait_ge(s["a_exped"], 1)
                dve.tensor_scalar(a_neg[:, :, :].rearrange("p k n -> p (k n)"), one_e[:, 0, 0:KH * NS], -1.0, None,
                                  ALU.mult).then_inc(s["a_set"], 1)
                dve.wait_ge(s["w_loaded"], 16 * W_LOADS)
                dve.tensor_scalar(omr[:, :], mur[:, :], -1.0, 1.0, ALU.mult, ALU.add).then_inc(s["omu_set"], 1)
                dve.tensor_scalar(omk[:, :], muk[:, :], -1.0, 1.0, ALU.mult, ALU.add).then_inc(s["omu_set"], 1)
                dve.wait_ge(s["ident_done"], 1)
                for h in range(KH):
                    dve.tensor_scalar(diag_d[:, h, :], ident[:, :], d_par[:, h:h + 1], None,
                                      ALU.mult).then_inc(s["diag_set"], 1)

            def stats(src, st, mv, ve, ln, count):
                for j in range(TB):
                    last = dve.bn_stats(st[:, j, :], src[:, j, :])
                last.then_inc(s[ln + "_stat"], 1)
                need(dve, s[ln + "_stat"], count)
                dve.sem_inc(s["dve_waited"], 1)
                for j in range(TB):
                    last = dve.bn_aggr(mv[:, j, :], st[:, j, :])
                last.then_inc(s[ln + "_mv"], 1)
                need(dve, s[ln + "_mv"], count)
                dve.tensor_scalar(ve, mv[:, :, 1], EPS, None, ALU.add).then_inc(s[ln + "_ve"], 1)

            def neg_mean(mv, rs, nm, rs_sem, count, ln):
                need(dve, s[rs_sem], count)
                dve.scalar_tensor_tensor(nm[:, :], mv[:, :, 0], -1.0, rs, ALU.mult,
                                         ALU.mult).then_inc(s[ln + "_nm"], 1)

            def times_b(i, ip, n):
                need(dve, b_loaded[n // GN], 16 * (i + 1))
                need(dve, s["u_done"], i + 1)
                need(dve, s["scan_done"], KH * (NS * i + n - X_RING + 1))
                dve.tensor_tensor(dbx[:, n % X_RING, :, :], u[:, ip, :, :], b_of(n),
                                  ALU.mult).then_inc(s["dbx_vec"], 1)

            def scans(t, n):
                cols, sem_of = (VEC_COLS, "dbx_vec") if n in VEC_COLS else (POOL_COLS, "dbx_pool")
                need(dve, s[sem_of], len(cols) * t + made(cols, n))
                need(dve, s["carry_saved"], NS * (t - 1) + n + 1)
                need(dve, s["y_added"], NS * t + n - H_RING + 1)
                for h in range(KH):
                    need(dve, s["da_ready"], KH * (NS * t + n) + h + 1)
                    dve.tensor_tensor_scan(hg[:, n % H_RING, h, :], da_ps[:, (KH * n + h) % DA_BANKS, :],
                                           dbx[:, n % X_RING, h, :], carry[:, n, h:h + 1],
                                           ALU.mult, ALU.add).then_inc(s["scan_done"], 1)

            def times_c(i, n):
                need(dve, c_loaded[n // GN], 16 * (i + 1))
                need(dve, s["carry_saved"], NS * i + n + 1)
                dve.tensor_tensor(hg[:, n % H_RING, :, :], hg[:, n % H_RING, :, :], c_of(n),
                                  ALU.mult).then_inc(s["g_last_ready"], 1)

            def step(t, par, pre=False, scan=False, mid=False, end=False, more=False):
                nxt = 1 - par

                def residual(v):
                    need(dve, s["post_ready"], post_count(t, f"wo{v}"))
                    need(dve, s["res_set"], t)
                    dve.tensor_tensor(res[:, 2 * v:2 * v + 2, :], by_block(post_bank(t, f"wo{v}")),
                                      res[:, 2 * v:2 * v + 2, :], ALU.add).then_inc(read_sem(t, f"wo{v}"), 1)

                def gate_v(v):
                    need(dve, s["sig_done"], t - 1)
                    need(dve, s["post_ready"], post_count(t, f"v{v}"))
                    dve.tensor_tensor(r_out[:, 2 * v:2 * v + 2, :], r_out[:, 2 * v:2 * v + 2, :],
                                      by_block(post_bank(t, f"v{v}")), ALU.mult).then_inc(read_sem(t, f"v{v}"), 1)

                def at(stage):
                    return n == turns(VEC_TURN, VEC_LAST, t)[stage]

                for n in range(NS):
                    ahead = column_at(t, par, n + 1, scan, pre, mid)
                    if ahead and ahead[2] in VEC_COLS:
                        times_b(*ahead)
                    if scan:
                        scans(t, n)
                    if n == 0 and scan and not (isinstance(t, int) and t == NT - 1):
                        dve.tensor_copy(keep[:, par:par + 1], notfirst[:, bass.ds(t + 1, 1)]).then_inc(s["keep_set"], 1)
                    behind = column_at(t, par, n - C_LAG, scan, pre, mid)
                    if behind and vec_c(behind[0], behind[2]):
                        times_c(behind[0], behind[2])
                    for mix, mu, stage, share, sums in ((xk, muk, "mix_k", "mixed_prev_k", "mixed_k"),
                                                        (xr, mur, "mix_r", "mixed_prev_r", "mixed_r")):
                        if end and at(stage):
                            need(dve, s[share], t - 1)
                            for k in range(KH):
                                last = dve.scalar_tensor_tensor(mix[:, k, :], hT[:, k, 1:LC + 1], mu[:, k:k + 1],
                                                                mix[:, k, :], ALU.mult, ALU.add)
                            last.then_inc(s[sums], 1)
                    if isinstance(t, int) and t == -1 and n == 0:
                        need(dve, s["x_loaded"], 16)
                        stats(x_tok, st1, mv1, ve13[:, 0, :], "ln1", 1)
                    if pre and at("nm1"):
                        neg_mean(mv1, rs13[:, 0, :], nm1, "ln13_rs", t + 2, "ln1")
                        if isinstance(t, int) and t == -1:
                            turned_weight(0, wxT)
                            small_constants()
                    if mid and at("gate"):
                        need(dve, s["y_added"], NS * t)
                        need(dve, s["z_done"], t)
                        dve.tensor_tensor(gated[:, :, :], y_ps[:, :, :], zs[:, nxt, :, :],
                                          ALU.mult).then_inc(s["gated_done"], 1)
                    for v in range(2):
                        if mid and at(f"res{v}"):
                            residual(v)
                    if mid and at("stats2"):
                        need_read(dve, t, "wo0")
                        need_read(dve, t, "wo1")
                        stats(res, st2, mv2, rs2[:, :], "ln2", t)
                    for v in range(2):
                        if end and at(f"gv{v}") and not (v == 1 and isinstance(t, int) and t == NT + 1):
                            gate_v(v)
                    if mid and at("nm2"):
                        neg_mean(mv2, rs2[:, :], nm2, "ln2_rs", t, "ln2")
                    if end and at("out"):
                        ended = isinstance(t, int) and t == NT + 1
                        for blocks in ([slice(0, TB // 2), slice(TB // 2, TB)] if ended else [slice(0, TB)]):
                            if ended and blocks.start:
                                gate_v(1)
                            need_read(dve, t, "v0")
                            if blocks.stop == TB:
                                need_read(dve, t, "v1")
                            dve.tensor_tensor(r_out[:, blocks, :], r_out[:, blocks, :], xres[:, par, blocks, :],
                                              ALU.add).then_inc(s["ffn_done"], 1)
                    if isinstance(t, int) and t == -1 and n == VEC_TURN["log1p"]:
                        turned_weight(1, w_dtx[:, :, :])
                    if pre and at("log1p"):
                        need(dve, s["ln_done"], t + 2)
                        dve.scalar_tensor_tensor(flat(one_e), flat(one_e), 1.0, flat(abs_v), ALU.subtract,
                                                 ALU.subtract).then_inc(s["nc_done"], 1)
                    if pre and at("relu"):
                        need(dve, s["nc_done"], t + 2)
                        need(dve, s["ln1_done"], 1)
                        dve.scalar_tensor_tensor(flat(relu_v), flat(relu_v), ln_of_1[:, 0:1], flat(one_e), ALU.subtract,
                                                 ALU.subtract).then_inc(s["rl_done"], 1)
                    if pre and at("delta"):
                        need(dve, s["rl_done"], t + 2)
                        dve.tensor_tensor(delta[:, nxt, :, :], relu_v[:, :, :], ln_v[:, :, :],
                                          ALU.add).then_inc(s["delta_done"], 1)
                    if pre and at("u"):
                        need(dve, s["delta_done"], t + 2)
                        dve.tensor_tensor(u[:, nxt, :, :], delta[:, nxt, :, :], xT[:, nxt, :, :],
                                          ALU.mult).then_inc(s["u_done"], 1)
                    if mid and at("gain"):
                        need(dve, s["res_normed"], t)
                        dve.tensor_tensor(res[:, :, :], res[:, :, :], g_all[:, :].unsqueeze(1).to_broadcast([P, TB, D]),
                                          ALU.mult).then_inc(s["ln2_g"], 1)
                    if mid and at("x2"):
                        need(dve, s["xb_done"], t)
                        need(dve, s["ln2_g"], t)
                        dve.tensor_tensor(xres[:, nxt, :, :], xres[:, nxt, :, :], res[:, :, :],
                                          ALU.add).then_inc(s["x2_done"], 1)
                    if mid and at("stats3"):
                        need(dve, s["x2_done"], t)
                        stats(xres[:, nxt, :, :], st3, mv3, ve13[:, 1, :], "ln3", t)
                    if pre and at("rs13"):
                        need(dve, s["rs_first_done"], t + 2)
                        first, step_ = ln13(rs_first, mid, more), ln13(rs_step, mid, more)
                        dve.scalar_tensor_tensor(step_, first, -0.5, first, ALU.mult, ALU.mult).then_inc(s["rs_sq"], 1)
                        need(dve, s["rs_sq"], t + 2)
                        dve.tensor_tensor(step_, step_, ln13(ve13, mid, more), ALU.mult).then_inc(s["rs_sqv"], 1)
                        need(dve, s["rs_sqv"], t + 2)
                        dve.scalar_tensor_tensor(ln13(rs13, mid, more), step_, 1.5, first, ALU.add,
                                                 ALU.mult).then_inc(s["ln13_rs"], 1)
                    if mid and at("nm3"):
                        neg_mean(mv3, rs13[:, 1, :], nm3, "ln13_rs", t + 3, "ln3")
                    if mid and at("hT_prev"):
                        need(dve, s["mixed_k"], t - 1)
                        need(dve, s["mixed_r"], t - 1)
                        dve.tensor_scalar(hT[:, :, 0], hT[:, :, LC], notfirst[:, bass.ds(t - 1, 1)], None,
                                          ALU.mult).then_inc(s["prev_done"], 1)
                    if more and at("stats1"):
                        need(dve, s["x_loaded"], 16 * (t + 3))
                        stats(x_tok, st1, mv1, ve13[:, 0, :], "ln1", t + 3)

            steps(dve, step)

        @block.tensor
        def _(pe):
            pe.wait_ge(s["ident_done"], 1)

            def turn_weight(m, src):
                dst = (pre_ps, post_ps)[m % 2]
                for k in range(KH):
                    for c in range(KH):
                        last = pe.transpose(dst[:, c * D + k * P:c * D + k * P + P], src[:, k, c * P:(c + 1) * P],
                                            ident[:, :])
                last.then_inc(s["setup_pe"], 1)

            pe.wait_ge(s["w_dt_loaded"], 32)
            turn_weight(0, wx_raw)

            def merge_dt_weights():
                pe.wait_ge(s["setup_ev"], 1)
                for m in range(KH):
                    for k in range(KH):
                        last = pe.matmul(post_ps[:, m * D:(m + 1) * D], wxT[:, k, m * P:(m + 1) * P], wdt_raw[:, k, :],
                                         start=k == 0, stop=k == KH - 1)
                last.then_inc(s["setup_pe"], 1)

            def turn_ffn_weights():
                pe.wait_ge(s["w_loaded"], 16 * W_LOADS)
                for m, src in enumerate(raw):
                    pe.wait_ge(s["setup_ev"], 1 + m)
                    turn_weight(2 + m, src)

            def add_up(i, n):
                if isinstance(i, int) and i == NT - 1:
                    need(pe, s["g_last_ready"], made(LAST_VEC_C, n))
                    need(pe, s["g_ready"], NS * i + n + 1 - made(LAST_VEC_C, n))
                else:
                    need(pe, s["g_ready"], NS * i + n + 1)
                if n == 0:
                    need(pe, s["gated_done"], i)
                for h in range(KH):
                    last = pe.matmul(y_ps[:, h, :], ident[:, :], hg[:, n % H_RING, h, :],
                                     start=n == 0, stop=n == NS - 1)
                last.then_inc(s["y_added"], 1)

            def project(out, w, x, cols):
                for k in range(KH):
                    last = pe.matmul(out, w[:, k, cols], x[:, k, :], start=k == 0, stop=k == KH - 1)
                return last

            def by_token(out, v, xT_, w):
                for b in range(2):
                    for k in range(KH):
                        tokens = slice((2 * v + b) * P, (2 * v + b + 1) * P)
                        last = pe.matmul(by_block(out)[:, b, :], xT_[:, k, tokens], w[:, k, :],
                                         start=k == 0, stop=k == KH - 1)
                return last

            def turned(bank, src, k):
                for j in range(TB):
                    last = pe.transpose(bank[:, j * P:(j + 1) * P], src[:, j, k * P:(k + 1) * P], ident[:, :])
                return last

            def step(t, par, pre=False, scan=False, mid=False, end=False, more=False):
                nxt = 1 - par
                i = t + 1

                def pre_unit(unit):
                    start = isinstance(t, int) and t == -1
                    need(pe, s["pre_read"], pre_count(i, unit) - (len(START_BANKS) if start else 1))
                    out = bank(t, unit)
                    m = int(unit[-1]) if unit != "bc" else 0
                    cols = slice(m * P, (m + 1) * P)
                    if unit in ("xnT0", "xnT1"):
                        need(pe, s["xn_done"], i + 1)
                        last = turned(out, xn_tok[:, nxt, :, :], m)
                    elif unit in ("x0", "x1"):
                        need(pe, s["pre_read"], pre_count(i, "xnT1"))
                        if start:
                            pe.wait_ge(s["w_in_loaded"], 16)
                        last = project(out[:, :], w_in, xnT, cols)
                    elif unit in ("z0", "z1"):
                        last = project(out[:, :], w_in, xnT, slice(D + m * P, D + (m + 1) * P))
                    elif unit == "bc":
                        if start:
                            merge_dt_weights()
                        need(pe, s["pre_read"], pre_count(i, "x1"))
                        if start:
                            pe.wait_ge(s["w_loaded"], 16 * W_LOADS)
                        last = project(out[0:2 * NS, :], w_bc, xT[:, nxt, :, :], slice(0, 2 * NS))
                    else:
                        if start:
                            pe.wait_ge(s["setup_ev"], 2)
                        last = project(out[:, :], w_dtx, xT[:, nxt, :, :], cols)
                    last.then_inc(s["pre_ready"], 1)

                def post_unit(unit):
                    if tail_index(t, unit) == 0:
                        pe.wait_ge(s["pre_read"], len(PRE) * NT)
                    else:
                        need_read(pe, t, unit, before=1 if tail_index(t, unit) is None else 2)
                    m = int(unit[-1])
                    cols = slice(m * P, (m + 1) * P)
                    out = post_bank(t, unit)
                    if unit[:2] == "wo":
                        need(pe, s["gated_done"], t)
                        last = by_token(out, m, gated, w_out)
                    elif unit[:2] == "hT":
                        need(pe, s["hn_done"], t)
                        last = turned(out, res, m)
                    elif unit[0] == "k":
                        need(pe, s["mixed_k"], t - 1)
                        last = project(out[:, :], w_kT, xk, cols)
                    elif unit[0] == "r":
                        need(pe, s["mixed_r"], t - 1)
                        last = by_token(out, m, xr, w_rT)
                    else:
                        need(pe, s["kact_done"], t - 1)
                        last = by_token(out, m, kact, w_vT)
                    last.then_inc(s["post_ready"], 1)

                for n in range(NS):
                    for unit in PRE + (POST_LAST if isinstance(t, int) and t == NT else POST):
                        if n == turns(PE_TURN, PE_LAST, t)[unit]:
                            if unit in PRE and pre:
                                pre_unit(unit)
                            if (unit in POST_A and mid) or (unit in POST_B and end):
                                post_unit(unit)
                    if scan and n == PE_TURN["xD"]:
                        if isinstance(t, int) and t == 0:
                            pe.wait_ge(s["diag_set"], KH)
                        for h in range(KH):
                            pe.matmul(y_ps[:, h, :], diag_d[:, h, :], xT[:, par, h, :], start=False, stop=False)
                    if isinstance(t, int) and t == -1 and n == PE_TURN["z1"]:
                        turn_ffn_weights()
                        pe.wait_ge(s["setup_ev"], 5)
                    behind = column_at(t, par, n - Y_LAG, scan, pre, mid)
                    if behind:
                        add_up(behind[0], behind[2])

            steps(pe, step)


_INS = ["L0_attn_x_in", "L0_attn_W_in", "L0_attn_W_x", "L0_attn_W_dt", "L0_attn_b_dt", "L0_attn_A_log",
        "L0_attn_D_param", "L0_attn_W_out", "L0_attn_ln_g", "L0_attn_ln_b", "L0_ffn_W_r", "L0_ffn_W_k",
        "L0_ffn_W_v", "L0_ffn_mu_r", "L0_ffn_mu_k"]
_OUT = ((BATCH, LEN, D), "float32")


def kernel(**inputs):
    import numpy as _np
    import concourse.bacc as _bacc
    from concourse import mybir as _mybir
    from concourse.bass_utils import run_bass_kernel_spmd as _run

    nc = _bacc.Bacc("TRN2", target_bir_lowering=False, num_devices=1)
    arrays, args = {}, []
    for name in _INS:
        a = _np.ascontiguousarray(inputs[name])
        arrays[f"in_{name}_dram"] = a
        args.append(nc.dram_tensor(f"in_{name}_dram", a.shape, _mybir.dt.from_np(a.dtype), kind="ExternalInput").ap())
    shape, dtype = _OUT
    args.append(nc.dram_tensor("out_0_dram", shape, _mybir.dt.from_np(_np.dtype(dtype)), kind="ExternalOutput").ap())
    mamba_rwkv_layer(nc, *args)
    r = _run(nc, [arrays], core_ids=[0])
    return r.results[0]["out_0_dram"]
```
